# Optimizing a Trainium2 kernel written in Bass

```python
import numpy as np
import jax
import jax.numpy as jnp

def _softmax(x, axis=-1):
    return jax.nn.softmax(x, axis=axis)

def _gelu(x):
    return jax.nn.gelu(x, approximate=True)

def _silu(x):
    return jax.nn.silu(x)

def _sigmoid(x):
    return jax.nn.sigmoid(x)

def _layernorm(x, axis=-1, eps=1e-05):
    m = jnp.mean(x, axis=axis, keepdims=True)
    v = jnp.var(x, axis=axis, keepdims=True)
    return (x - m) / jnp.sqrt(v + eps)

def _scatter_add(tgt, idx, src, axis=0):
    return tgt.at[idx].add(src)

def _segment_sum(src, seg, n):
    return jax.ops.segment_sum(src, seg, n)
kernel_name = 'mk_prb_d1_jaxref_r8_b42707'

def setup_inputs(seed: int=0):
    np.random.seed(seed)
    _w = jnp.asarray

    def _L0_attn_setup():
        import jax, jax.numpy as jnp
        import numpy as np
        B, T, D, R = (4, 256, 128, 32)
        key = jax.random.key(seed)
        kx, ku = jax.random.split(key)
        x = jax.random.normal(kx, (B, T, D), dtype=jnp.float32)
        U = jax.random.normal(ku, (D, R), dtype=jnp.float32) * 0.05
        return {'x': x, 'U': U}
    _L0_attn_in = _L0_attn_setup()

    def _L0_ffn_setup():
        import jax, jax.numpy as jnp
        import numpy as np
        B, S, H = (4, 256, 128)
        E, K = (8, 2)
        I_R, I_S = (4 * H, 8 * H)
        CAP_FACTOR = 1.25
        SCALE = 1.0
        key = jax.random.key(seed)
        ks = jax.random.split(key, 9)
        std = 0.02
        return {'x': jax.random.normal(ks[0], (B, S, H), jnp.float32), 'router_w': std * jax.random.normal(ks[1], (E, H), jnp.float32), 'rg': std * jax.random.normal(ks[2], (E, H, I_R), jnp.float32), 'ru': std * jax.random.normal(ks[3], (E, H, I_R), jnp.float32), 'rd': std * jax.random.normal(ks[4], (E, I_R, H), jnp.float32), 'sg': std * jax.random.normal(ks[5], (H, I_S), jnp.float32), 'su': std * jax.random.normal(ks[6], (H, I_S), jnp.float32), 'sd': std * jax.random.normal(ks[7], (I_S, H), jnp.float32)}
    _L0_ffn_in = _L0_ffn_setup()
    _d = {'L0_attn_x': _L0_attn_in['x'], 'L0_attn_U': _L0_attn_in['U'], 'L0_ffn_router_w': _L0_ffn_in['router_w'], 'L0_ffn_rg': _L0_ffn_in['rg'], 'L0_ffn_ru': _L0_ffn_in['ru'], 'L0_ffn_rd': _L0_ffn_in['rd'], 'L0_ffn_sg': _L0_ffn_in['sg'], 'L0_ffn_su': _L0_ffn_in['su'], 'L0_ffn_sd': _L0_ffn_in['sd']}
    _x0 = _d['L0_attn_x']
    _d['L0_attn_x'] = jax.random.normal(jax.random.fold_in(jax.random.key(seed), 1), (4, 512, 128), dtype=_x0.dtype)
    del _x0
    return _d

def reference(L0_attn_x, L0_attn_U, L0_ffn_router_w, L0_ffn_rg, L0_ffn_ru, L0_ffn_rd, L0_ffn_sg, L0_ffn_su, L0_ffn_sd):

    def _L0_attn_ref(x, U):
        import jax, jax.numpy as jnp
        import numpy as np
        B, T, D, R = (4, 256, 128, 32)
        y = jnp.einsum('btd,dr->btr', x, U)
        n = jnp.sum(y * y, axis=-1)
        cross = jnp.einsum('btr,bjr->btj', y, y)
        dist_sq = n[:, :, None] + n[:, None, :] - 2.0 * cross
        attn = jax.nn.softmax(-dist_sq, axis=-1)
        return jnp.einsum('btj,bjd->btd', attn, x)

    def _L0_ffn_ref(x, router_w, rg, ru, rd, sg, su, sd):
        import jax, jax.numpy as jnp
        import numpy as np
        B, S, H = (4, 256, 128)
        E, K = (8, 2)
        I_R, I_S = (4 * H, 8 * H)
        CAP_FACTOR = 1.25
        SCALE = 1.0
        b, s, h = x.shape
        T = b * s
        capacity = max(int(CAP_FACTOR * T / E), 1)
        xf = x.reshape(T, h)
        eps = jnp.finfo(x.dtype).eps
        xn = xf * jax.lax.rsqrt(jnp.mean(xf * xf, axis=-1, keepdims=True) + eps)
        logits = xn @ router_w.T
        probs = jax.nn.softmax(logits, axis=-1)
        topk_p, topk_i = jax.lax.top_k(probs, K)
        rw = topk_p / jnp.sum(topk_p, axis=-1, keepdims=True)
        one_hot = jax.nn.one_hot(topk_i, E, dtype=x.dtype)
        mask = one_hot.sum(1)
        wdense = (one_hot * rw[..., None]).sum(1)
        sel = mask.T.astype(bool)
        order = jnp.argsort(~sel, axis=1, stable=True)
        dispatch = order[:, :capacity]
        count = sel.sum(axis=1)
        valid = (jnp.arange(capacity)[None, :] < count[:, None]).astype(x.dtype)
        xg = xf[dispatch]
        gate = jax.nn.silu(jnp.einsum('ech,ehi->eci', xg, rg))
        up = jnp.einsum('ech,ehi->eci', xg, ru)
        eout = jnp.einsum('eci,eih->ech', gate * up, rd)
        w = jnp.take_along_axis(wdense.T, dispatch, axis=1)
        contrib = eout * (w * valid)[..., None]
        routed = jnp.zeros_like(xf).at[dispatch.reshape(-1)].add(contrib.reshape(-1, h))
        shared = jax.nn.silu(x @ sg) * (x @ su) @ sd
        return shared + SCALE * routed.reshape(b, s, h)
    x = L0_attn_x
    xn = _layernorm(x, axis=-1)
    x = x + _L0_attn_ref(xn, L0_attn_U) + _L0_ffn_ref(xn, L0_ffn_router_w, L0_ffn_rg, L0_ffn_ru, L0_ffn_rd, L0_ffn_sg, L0_ffn_su, L0_ffn_sd)
    return x

_drawn_inputs = setup_inputs


def setup_inputs(seed=0):
    import zlib

    import numpy as np

    out = dict(_drawn_inputs(seed))
    spreads = {}
    factors = {'L0_attn_U': 8.0,
     'L0_ffn_router_w': 8.0,
     'L0_ffn_rg': 8.0,
     'L0_ffn_ru': 8.0,
     'L0_ffn_rd': 8.0,
     'L0_ffn_sg': 6.802,
     'L0_ffn_su': 6.762,
     'L0_ffn_sd': 6.765}
    for name, (base, spread) in spreads.items():
        noise = np.random.default_rng([zlib.crc32(name.encode()), seed]).standard_normal(out[name].shape)
        drawn = base * np.exp(spread * noise) if base else spread * noise
        out[name] = jnp.asarray(drawn.astype(out[name].dtype))
    for name, factor in factors.items():
        out[name] = (out[name] * factor).astype(out[name].dtype)
    return out
```

```python
from contextlib import ExitStack

import concourse.bass as bass
from concourse import mybir

ALU = mybir.AluOpType
ACT = mybir.ActivationFunctionType
AX_X = mybir.AxisListType.X
F32 = mybir.dt.float32
F32R = mybir.dt.float32r
BF16 = mybir.dt.bfloat16
I32 = mybir.dt.int32

P = 128
LN_EPS = 1e-5
RMS_EPS = 1.1920928955078125e-07
CAP_FACTOR = 1.25
TOP_K = 2


def moe_attention_kernel(nc, x_in, U_in, rw_in, rg_in, ru_in, rd_in, sg_in, su_in, sd_in, out):
    B, S, D = x_in.shape
    R = U_in.shape[1]
    E, _, IR = rg_in.shape
    IS = sg_in.shape[1]
    assert D == P and S == 512 and R == 32 and TOP_K == 2
    T = B * S
    NT = T // P
    TG = S // P
    CAP = max(int(CAP_FACTOR * T / E), 1)
    CR = IR // P
    CS = IS // P
    ZROW = E * CAP
    TAIL = CAP - 2 * P
    assert 0 < TAIL <= P and E <= 8
    EARLY = 2
    ZCH = E * CAP // P

    def block_job(b):
        return b if b < EARLY else b + E

    def block_chunk(b):
        return CS * b if b < EARLY else CS * b + CR * E

    def expert_job(e):
        return EARLY + e

    def expert_chunk(e):
        return CS * EARLY + CR * e

    slots_dram = nc.dram_tensor("slots_dram", (E * CAP, D), F32).ap()
    eout_dram = nc.dram_tensor("eout_dram", (E * CAP + 1, D), F32).ap()

    x_v = x_in.rearrange("b (t p) d -> b p t d", p=P)
    out_v = out.rearrange("b (t p) d -> b p t d", p=P)

    def slot_rows(dram, e):
        lo = e * CAP
        return (dram[lo:lo + 2 * P, :].rearrange("(p r) d -> p r d", r=2),
                dram[lo + 2 * P:lo + CAP, :])

    with ExitStack() as ctx:
        def sb(name, shape, dt=F32):
            return ctx.enter_context(nc.sbuf_tensor(name, shape, dt))

        def sem(name):
            return ctx.enter_context(nc.semaphore(name))

        acc = sb("acc", [P, NT, D])
        xn = sb("xn", [P, NT, D + 1])
        xnT_hi = sb("xnT_hi", [P, T], F32R)
        xnT_lo = sb("xnT_lo", [P, T], F32R)
        ident = sb("ident", [P, P])
        zeros = sb("zeros", [P, D])
        tri = sb("tri", [P, P], BF16)
        ones_bf = sb("ones_bf", [P, P], BF16)
        ones_f = sb("ones_f", [P, P])
        e_ids = sb("e_ids", [P, E])
        e_ids_i = sb("e_ids_i", [P, E], I32)
        part_i = sb("part_i", [P, 1], I32)
        row97 = sb("row97", [P, 1])
        seg = sb("seg", [P, E * NT])
        slot0 = sb("slot0", [P, E])
        half = sb("half", [R, 2])
        rw_raw = sb("rw_raw", [E, D])
        rwT = sb("rwT", [P, 2 * E], F32R)
        U_raw = sb("U_raw", [P, R])
        U_hi = sb("U_hi", [P, 3, R], F32R)
        U_lo = sb("U_lo", [P, 3, R], F32R)
        yL = sb("yL", [P, T], F32R)
        yR = sb("yR", [P, T], F32R)
        ysq = sb("ysq", [R, T])
        nhi = sb("nhi", [P, S], F32R)
        nbias = sb("nbias", [P, NT])
        rden = sb("rden", [P, NT])
        stats = sb("stats", [P, NT, 6])
        mv = sb("mv", [P, NT, 2])
        ve = sb("ve", [P, NT])
        std = sb("std", [P, NT])
        r0 = sb("r0", [P, NT])
        nt_a = sb("nt_a", [P, NT])
        nt_b = sb("nt_b", [P, NT])
        rstd = sb("rstd", [P, NT])
        ms = sb("ms", [P, NT])
        rms_s = sb("rms_s", [P, NT])
        rms_0 = sb("rms_0", [P, NT])
        rms = sb("rms", [P, NT])
        lg = sb("lg", [P, NT, 2 * E])
        z = sb("z", [P, NT, E])
        z2 = sb("z2", [P, NT, E])
        key = sb("key", [P, NT, E])
        oh1 = sb("oh1", [P, NT, E])
        oh2 = sb("oh2", [P, NT, E])
        sel = sb("sel", [P, E, NT], BF16)
        m1 = sb("m1", [P, NT])
        m2 = sb("m2", [P, NT])
        i1 = sb("i1", [P, NT])
        i2 = sb("i2", [P, NT])
        e2 = sb("e2", [P, NT])
        e2p = sb("e2p", [P, NT])
        wgt = sb("wgt", [P, 2, NT])
        incl = sb("incl", [P, E, NT])
        base = sb("base", [P, E, NT])
        pos = sb("pos", [P, E, NT])
        over = sb("over", [P, E, NT])
        slot = sb("slot", [P, E, NT])
        pick = sb("pick", [P, 2, NT, E])
        slot_f = sb("slot_f", [P, 2, NT])
        slot_i = sb("slot_i", [P, 2, NT], I32)
        sw_raw = sb("sw_raw", [P, 2, IS])
        sw_hi = sb("sw_hi", [P, 2, IS], F32R)
        sw_lo = sb("sw_lo", [P, 2, IS], F32R)
        sd = sb("sd", [P, CS, D])
        ew_raw = sb("ew_raw", [P, 2, 2, IR])
        ew_hi = sb("ew_hi", [P, 2, 2, IR], F32R)
        ew_lo = sb("ew_lo", [P, 2, 2, IR], F32R)
        rd = sb("rd", [P, 3, CR, D])
        xg = sb("xg", [P, 2, 3, D])
        xgT_hi = sb("xgT_hi", [P, 2, CAP], F32R)
        xgT_lo = sb("xgT_lo", [P, 2, CAP], F32R)
        silu = sb("silu", [P, 2, S])
        hid_s = sb("hid_s", [P, 2, CS, S])
        assert CS == 2 * TG
        probs = hid_s[:, 1, :, :].rearrange("p (b j) i -> p b j i", b=2)
        hid_e = sb("hid_e", [P, 2, CR, CAP])
        eo = sb("eo", [P, 2, 3, D])
        got = sb("got", [P, NT, 2, D])

        bank = [ctx.enter_context(nc.psum_tensor(f"bank{i}", [P, 512], F32)) for i in range(8)]
        gate_b = [bank[0], bank[2]]
        up_b = [bank[1], bank[3]]
        down_b = [bank[4], bank[5]]
        turn_b = [bank[6], bank[7]]
        nb_ps = bank[4]
        rw_ps = bank[4][:, 64:64 + E]
        lg_ps = bank[5][:, 0:NT * 2 * E].rearrange("p (t c) -> p t c", t=NT)
        rank_ps = bank[6][:, 0:E * NT].rearrange("p (e t) -> p e t", e=E)
        tot_ps = bank[7][:, 0:E * NT]

        x_in_s = [sem(f"x_loaded{g}") for g in range(B)]
        rw_loaded, U_loaded = sem("rw_loaded"), sem("U_loaded")
        sw_loaded, sd_loaded = sem("sw_loaded"), sem("sd_loaded")
        ew_loaded = [sem(f"ew_loaded{i}") for i in range(2)]
        rd_loaded = [sem(f"rd_loaded{i}") for i in range(3)]
        xg_loaded = [sem(f"xg_loaded{i}") for i in range(2)]
        zero_filled = sem("zero_filled")
        scattered = sem("scattered")
        eo_written = [sem(f"eo_written{i}") for i in range(2)]
        gathered = [sem(f"gathered{t}") for t in range(NT)]
        out_written = sem("out_written")
        pool_step = sem("pool_step")
        consts = sem("consts")
        zeros_set = sem("zeros_set")
        dve_const = sem("dve_const")
        dve_step = sem("dve_step")
        ve_ready = sem("ve_ready")
        std_ready = sem("std_ready")
        xn_ready = sem("xn_ready")
        ms_ready = sem("ms_ready")
        rms_ready = sem("rms_ready")
        rwT_turned, rwT_hi_s, rwT_ready = sem("rwT_turned"), sem("rwT_hi_s"), sem("rwT_ready")
        U_hi_s, U_ready = sem("U_hi_s"), sem("U_ready")
        xnT_turned, xnT_hi_s, xnT_ready = sem("xnT_turned"), sem("xnT_hi_s"), sem("xnT_ready")
        lg_done, lg_copied = sem("lg_done"), sem("lg_copied")
        y_done, y_hi_s, y_ready = sem("y_done"), sem("y_hi_s"), sem("y_ready")
        ysq_ready, n_done, nhi_ready = sem("ysq_ready"), sem("n_done"), sem("nhi_ready")
        nb_copied = sem("nb_copied")
        e2_asked, e2_ready = sem("e2_asked"), sem("e2_ready")
        sel_ready, rank_done = sem("sel_ready"), sem("rank_done")
        pos_ready = sem("pos_ready")
        slots_ready = sem("slots_ready")
        score_done, prob_ready = sem("score_done"), sem("prob_ready")
        att_done, att_added = sem("att_done"), sem("att_added")
        sw_hi_s, sw_ready = sem("sw_hi_s"), sem("sw_ready")
        ew_hi_s, ew_ready = sem("ew_hi_s"), sem("ew_ready")
        xg_turned, xg_hi_s, xg_ready = sem("xg_turned"), sem("xg_hi_s"), sem("xg_ready")
        chunk_done, silu_ready, hid_ready = sem("chunk_done"), sem("silu_ready"), sem("hid_ready")
        job_done = sem("job_done")
        block_added, eo_ready = sem("block_added"), sem("eo_ready")
        summed = sem("summed")

        block = ctx.enter_context(nc.Block())

        @block.sync
        def _(sp):
            def load_expert_weights(e, s):
                sp.dma_start(ew_raw[:, s, 0, :], rg_in[e]).then_inc(ew_loaded[s], 16)
                sp.dma_start(ew_raw[:, s, 1, :], ru_in[e]).then_inc(ew_loaded[s], 16)

            def load_down(e, s):
                sp.dma_start(rd[:, s, :, :], rd_in[e].rearrange("(c p) d -> p c d", p=P)
                             ).then_inc(rd_loaded[s], 16)

            def load_slots(e, s):
                main, tail = slot_rows(slots_dram, e)
                sp.dma_start(xg[:, s, 0:2, :], main).then_inc(xg_loaded[s], 16)
                sp.dma_start(xg[0:TAIL, s, 2, :], tail).then_inc(xg_loaded[s], 16)

            for g in range(B):
                sp.dma_start(acc[:, TG * g:TG * g + TG, :], x_v[g]).then_inc(x_in_s[g], 16)
                if g == 0:
                    sp.dma_start(rw_raw[:, :], rw_in).then_inc(rw_loaded, 16)
                    sp.dma_start(U_raw[:, :], U_in).then_inc(U_loaded, 16)
            sp.wait_ge(zeros_set, 1)
            sp.dma_start(slots_dram.rearrange("(p a) d -> p a d", p=P),
                         zeros[:, :].rearrange("p (o d) -> p o d", o=1).to_broadcast([P, ZCH, D])
                         ).then_inc(zero_filled, 16)
            sp.dma_start(eout_dram[ZROW:ZROW + 1, :], zeros[0:1, 0:D]).then_inc(zero_filled, 16)
            sp.dma_start(sw_raw[:, 0, :], sg_in).then_inc(sw_loaded, 16)
            sp.dma_start(sw_raw[:, 1, :], su_in).then_inc(sw_loaded, 16)
            sp.dma_start(sd[:, :, :], sd_in.rearrange("(c p) d -> p c d", p=P)).then_inc(sd_loaded, 16)
            for e in range(2):
                load_expert_weights(e, e)
                load_down(e, e)
            sp.wait_ge(scattered, 16 * 2 * NT)
            for e in range(2):
                load_slots(e, e)
            for e in range(E - 2):
                sp.wait_ge(ew_ready, e + 1)
                load_expert_weights(e + 2, e % 2)
                sp.wait_ge(xg_turned, e + 1)
                load_slots(e + 2, e % 2)
                sp.wait_ge(job_done, expert_job(e - 1) + 1)
                load_down(e + 2, (e + 2) % 3)
            for g in range(B):
                sp.wait_ge(summed, TG * (g + 1))
                sp.dma_start(out_v[g], acc[:, TG * g:TG * g + TG, :]).then_inc(out_written, 16)
            sp.wait_ge(out_written, 16 * B)

        @block.gpsimd
        def _(pool):
            steps = [0]

            def after(ins):
                steps[0] += 1
                ins.then_inc(pool_step, 1)
                pool.wait_ge(pool_step, steps[0])

            after(nc.gpsimd.memset(ones_f[:, :], 1.0))
            after(nc.gpsimd.affine_select(out=ident[:, :], in_=ones_f[:, :], compare_op=ALU.is_equal,
                                          fill=0.0, base=0, pattern=[[-1, P]], channel_multiplier=1))
            after(nc.gpsimd.affine_select(out=tri[:, :], in_=ones_f[:, :], compare_op=ALU.is_gt,
                                          fill=0.0, base=0, pattern=[[1, P]], channel_multiplier=-1))
            after(nc.gpsimd.iota(e_ids_i[:, :], pattern=[[1, E]], base=0, channel_multiplier=0))
            after(nc.gpsimd.iota(part_i[:, :], pattern=[[0, 1]], base=0, channel_multiplier=1))
            nc.gpsimd.affine_select(out=seg[:, :].rearrange("p (e t) -> p e t", e=E),
                                    in_=ones_f[:, 0:E * NT].rearrange("p (e t) -> p e t", e=E),
                                    compare_op=ALU.is_gt, fill=0.0, base=0,
                                    pattern=[[0, E], [1, NT]], channel_multiplier=0).then_inc(consts, 1)
            pool.wait_ge(zero_filled, 32)
            pool.wait_ge(xn_ready, B)
            pool.wait_ge(slots_ready, 1)
            for t in range(NT):
                for k in range(2):
                    nc.gpsimd.indirect_dma_start(
                        slots_dram, bass.IndirectOffsetOnAxis(slot_i[:, k, t:t + 1], 0), xn[:, t, 0:D], None,
                        bounds_check=E * CAP - 1, oob_is_err=False).then_inc(scattered, 16)
            for e in range(E):
                main, tail = slot_rows(eout_dram, e)
                pool.wait_ge(eo_ready, e + 1)
                nc.gpsimd.dma_start(main, eo[:, e % 2, 0:2, :]).then_inc(eo_written[e % 2], 16)
                nc.gpsimd.dma_start(tail, eo[0:TAIL, e % 2, 2, :]).then_inc(eo_written[e % 2], 16)
            for s in range(2):
                pool.wait_ge(eo_written[s], 32 * (E // 2))
            for t in range(NT):
                for k in range(2):
                    nc.gpsimd.indirect_dma_start(
                        got[:, t, k, :], None, eout_dram, bass.IndirectOffsetOnAxis(slot_i[:, k, t:t + 1], 0),
                        bounds_check=ZROW, oob_is_err=False).then_inc(gathered[t], 16)

        @block.scalar
        def _(act):
            def turned_hi(g):
                act.wait_ge(xnT_turned, g + 1)
                nc.scalar.copy(xnT_hi[:, S * g:S * g + S], turn_b[g % 2][:, :]).then_inc(xnT_hi_s, 1)

            act.wait_ge(U_loaded, 16)
            for j in range(3):
                last = nc.scalar.copy(U_hi[:, j, :], U_raw[:, :])
            last.then_inc(U_hi_s, 1)
            act.wait_ge(rwT_turned, 1)
            nc.scalar.copy(rwT[:, 0:E], rw_ps).then_inc(rwT_hi_s, 1)
            for g in range(B):
                cols = slice(S * g, S * g + S)
                act.wait_ge(ve_ready, g + 1)
                nc.scalar.activation(std[:, TG * g:TG * g + TG], ve[:, TG * g:TG * g + TG], ACT.Sqrt
                                     ).then_inc(std_ready, 1)
                if g > 0:
                    turned_hi(g - 1)
            turned_hi(B - 1)
            act.wait_ge(ms_ready, 1)
            nc.scalar.activation(rms_s[:, :], ms[:, :], ACT.Sqrt).then_inc(rms_ready, 1)
            for g in range(B):
                cols = slice(S * g, S * g + S)
                act.wait_ge(y_done, g + 1)
                nc.scalar.copy(yL[0:3 * R, cols], bank[g][0:3 * R, :])
                nc.scalar.copy(yR[0:3 * R, cols], bank[g][0:3 * R, :]).then_inc(y_hi_s, 1)
                nc.scalar.activation(ysq[:, cols], bank[g][0:R, :], ACT.Square).then_inc(ysq_ready, 1)
            act.wait_ge(lg_done, B)
            nc.scalar.copy(lg[:, :, :], lg_ps).then_inc(lg_copied, 1)
            for g in range(B):
                act.wait_ge(n_done, g + 1)
                if g > 0:
                    act.wait_ge(y_ready, g)
                nc.scalar.copy(nhi[3 * R:3 * R + 2, :], bank[g][3 * R:3 * R + 2, :]).then_inc(nhi_ready, 1)
            nc.scalar.mul(nbias[:, :], nb_ps[:, 0:2 * NT].rearrange("p (t c) -> p t c", c=2)[:, :, 0], 2.0
                          ).then_inc(nb_copied, 1)
            act.wait_ge(nb_copied, 1)
            for b in range(B):
                for j in range(TG):
                    act.wait_ge(score_done, TG * b + j + 1)
                    if b >= 2:
                        act.wait_ge(att_done, 2 * (b - 1))
                    t = TG * b + j
                    nc.scalar.activation(probs[:, b % 2, j, :], bank[j][:, :], ACT.Exp,
                                         bias=nbias[:, t:t + 1], scale=2.0).then_inc(prob_ready, 1)
                if b == 0:
                    act.wait_ge(e2_asked, 1)
                    nc.scalar.activation(e2[:, :], m2[:, :], ACT.Exp).then_inc(e2_ready, 1)
                    act.wait_ge(sw_loaded, 32)
                    for w in range(2):
                        last = nc.scalar.copy(sw_hi[:, w, :], sw_raw[:, w, :])
                    last.then_inc(sw_hi_s, 1)

            def silu_chunk(q, n):
                act.wait_ge(chunk_done, q + 1)
                if q >= 2:
                    act.wait_ge(hid_ready, q - 1)
                nc.scalar.activation(silu[:, q % 2, 0:n], gate_b[q % 2][:, 0:n], ACT.Silu
                                     ).then_inc(silu_ready, 1)

            def split_weights(e):
                act.wait_ge(ew_loaded[e % 2], 32 * (e // 2 + 1))
                if e >= 2:
                    act.wait_ge(chunk_done, expert_chunk(e - 1))
                nc.scalar.copy(ew_hi[:, e % 2, :, :], ew_raw[:, e % 2, :, :]).then_inc(ew_hi_s, 1)

            def slots_hi(e):
                act.wait_ge(xg_turned, e + 1)
                if e >= 2:
                    act.wait_ge(chunk_done, expert_chunk(e - 1))
                nc.scalar.copy(xgT_hi[:, e % 2, :], turn_b[e % 2][:, 0:CAP]).then_inc(xg_hi_s, 1)

            def expert_out(e):
                act.wait_ge(job_done, expert_job(e) + 1)
                if e >= 2:
                    act.wait_ge(eo_written[e % 2], 32 * (e // 2))
                o = down_b[expert_job(e) % 2]
                nc.scalar.copy(eo[:, e % 2, 0:2, :], o[:, 0:2 * D].rearrange("p (r d) -> p r d", r=2))
                nc.scalar.copy(eo[0:TAIL, e % 2, 2, :], o[0:TAIL, 2 * D:3 * D]).then_inc(eo_ready, 1)

            for b in range(EARLY):
                for c in range(CS):
                    silu_chunk(block_chunk(b) + c, S)
                    if b == EARLY - 1 and c == CS // 2:
                        split_weights(0)
            slots_hi(0)
            for e in range(E):
                if e + 1 < E:
                    slots_hi(e + 1)
                for c in range(CR):
                    silu_chunk(expert_chunk(e) + c, CAP)
                    if c == 0 and e + 1 < E:
                        split_weights(e + 1)
                if e >= 1:
                    expert_out(e - 1)
            for b in range(EARLY, B):
                for c in range(CS):
                    silu_chunk(block_chunk(b) + c, S)
                    if b == EARLY and c == 1:
                        expert_out(E - 1)

        @block.vector
        def _(dve):
            steps = [0]

            def then(ins):
                steps[0] += 1
                ins.then_inc(dve_step, 1)
                dve.wait_ge(dve_step, steps[0])

            V = nc.vector
            V.memset(zeros[:, :], 0.0).then_inc(zeros_set, 1)
            V.memset(half[:, :], -0.5)
            V.memset(ones_bf[:, :], 1.0)
            V.memset(xn[:, :, D:D + 1], 1.0)
            V.memset(yL[3 * R:3 * R + 2, :].bitcast(F32), 1.0).then_inc(dve_const, 1)
            dve.wait_ge(consts, 1)
            V.tensor_copy(e_ids[:, :], e_ids_i[:, :])
            then(V.tensor_scalar(row97[:, :], part_i[:, :], float(3 * R + 1), -1.0, ALU.is_equal, ALU.mult))
            V.tensor_scalar(slot0[:, :], e_ids[:, :], float(CAP), None, ALU.mult)

            def stats_of(g):
                ts = slice(TG * g, TG * g + TG)
                dve.wait_ge(x_in_s[g], 16)
                for t in range(TG * g, TG * g + TG):
                    last = V.bn_stats(stats[:, t, :], acc[:, t, :])
                then(last)
                for t in range(TG * g, TG * g + TG):
                    last = V.bn_aggr(mv[:, t, :], stats[:, t, :])
                then(last)
                V.tensor_scalar(ve[:, ts], mv[:, ts, 1], LN_EPS, None, ALU.add).then_inc(ve_ready, 1)

            def newton(r, v, s, tmp_a, tmp_b, r_0):
                then(V.reciprocal(r_0, s))
                then(V.tensor_tensor(tmp_a, r_0, r_0, ALU.mult))
                then(V.tensor_tensor(tmp_b, tmp_a, v, ALU.mult))
                then(V.tensor_scalar(tmp_a, tmp_b, -0.5, 1.5, ALU.mult, ALU.add))
                then(V.tensor_tensor(r, tmp_a, r_0, ALU.mult))

            def normalize(g):
                ts = slice(TG * g, TG * g + TG)
                dve.wait_ge(std_ready, g + 1)
                newton(rstd[:, ts], ve[:, ts], std[:, ts], nt_a[:, ts], nt_b[:, ts], r0[:, ts])
                for t in range(TG * g, TG * g + TG):
                    last = V.tensor_scalar(xn[:, t, 0:D], acc[:, t, :], mv[:, t, 0:1], rstd[:, t:t + 1],
                                           ALU.subtract, ALU.mult)
                last.then_inc(xn_ready, 1)

            def turned_lo(g):
                cols = slice(S * g, S * g + S)
                dve.wait_ge(xnT_hi_s, g + 1)
                V.tensor_tensor(xnT_lo[:, cols], turn_b[g % 2][:, :], xnT_hi[:, cols].bitcast(F32),
                                ALU.subtract).then_inc(xnT_ready, 1)

            stats_of(0)
            normalize(0)
            dve.wait_ge(U_hi_s, 1)
            for j in range(3):
                last = V.tensor_tensor(U_lo[:, j, :], U_raw[:, :], U_hi[:, j, :].bitcast(F32), ALU.subtract)
            last.then_inc(U_ready, 1)
            dve.wait_ge(rwT_hi_s, 1)
            V.tensor_tensor(rwT[:, E:2 * E], rw_ps, rwT[:, 0:E].bitcast(F32), ALU.subtract
                            ).then_inc(rwT_ready, 1)
            for g in range(1, B):
                stats_of(g)
                normalize(g)
                turned_lo(g - 1)
            turned_lo(B - 1)
            then(V.tensor_tensor(nt_a[:, :], rstd[:, :], rstd[:, :], ALU.mult))
            then(V.tensor_tensor(nt_b[:, :], nt_a[:, :], mv[:, :, 1], ALU.mult))
            V.tensor_scalar(ms[:, :], nt_b[:, :], RMS_EPS, None, ALU.add).then_inc(ms_ready, 1)
            dve.wait_ge(rms_ready, 1)
            newton(rms[:, :], ms[:, :], rms_s[:, :], nt_a[:, :], nt_b[:, :], rms_0[:, :])
            for g in range(B):
                cols = slice(S * g, S * g + S)
                dve.wait_ge(y_hi_s, g + 1)
                V.tensor_tensor(yR[R:2 * R, cols], bank[g][R:2 * R, :], yL[R:2 * R, cols].bitcast(F32),
                                ALU.subtract)
                V.tensor_tensor(yL[2 * R:3 * R, cols], bank[g][2 * R:3 * R, :],
                                yR[2 * R:3 * R, cols].bitcast(F32), ALU.subtract)
                dve.wait_ge(nhi_ready, g + 1)
                V.scalar_tensor_tensor(out=yR[3 * R:3 * R + 2, cols], in0=nhi[3 * R:3 * R + 2, :].bitcast(F32),
                                       scalar=row97[3 * R:3 * R + 2, 0:1], in1=bank[g][3 * R:3 * R + 2, :],
                                       op0=ALU.mult, op1=ALU.add).then_inc(y_ready, 1)

            def per_token(ap):
                return ap.rearrange("p (t o) -> p t o", o=1).to_broadcast([P, NT, E])

            ids = e_ids[:, :].rearrange("p (o e) -> p o e", o=1).to_broadcast([P, NT, E])
            dve.wait_ge(lg_copied, 1)
            then(V.tensor_tensor(z2[:, :, :], lg[:, :, 0:E], lg[:, :, E:2 * E], ALU.add))
            then(V.tensor_tensor(z[:, :, :], z2[:, :, :], per_token(rms[:, :]), ALU.mult))
            then(V.tensor_reduce(m1[:, :], z[:, :, :], AX_X, ALU.max))
            then(V.tensor_tensor(z2[:, :, :], z[:, :, :], per_token(m1[:, :]), ALU.subtract))
            then(V.tensor_scalar(z[:, :, :], z2[:, :, :], -87.5, None, ALU.max))
            then(V.tensor_scalar(z2[:, :, :], z[:, :, :], 0.0, float(E), ALU.is_lt, ALU.mult))
            then(V.tensor_tensor(key[:, :, :], z2[:, :, :], ids, ALU.add))
            then(V.tensor_reduce(i1[:, :], key[:, :, :], AX_X, ALU.min))
            then(V.tensor_tensor(oh1[:, :, :], ids, per_token(i1[:, :]), ALU.is_equal))
            then(V.scalar_tensor_tensor(out=z2[:, :, :], in0=oh1[:, :, :], scalar=-1000.0, in1=z[:, :, :],
                                        op0=ALU.mult, op1=ALU.add))
            V.tensor_reduce(m2[:, :], z2[:, :, :], AX_X, ALU.max).then_inc(e2_asked, 1)
            dve.wait_ge(e2_asked, 1)
            then(V.tensor_tensor(key[:, :, :], z2[:, :, :], per_token(m2[:, :]), ALU.is_lt))
            then(V.tensor_scalar(z2[:, :, :], key[:, :, :], float(E), None, ALU.mult))
            then(V.tensor_tensor(key[:, :, :], z2[:, :, :], ids, ALU.add))
            then(V.tensor_reduce(i2[:, :], key[:, :, :], AX_X, ALU.min))
            then(V.tensor_tensor(oh2[:, :, :], ids, per_token(i2[:, :]), ALU.is_equal))
            V.tensor_tensor(sel[:, :, :].rearrange("p e t -> p t e"), oh1[:, :, :], oh2[:, :, :], ALU.add
                            ).then_inc(sel_ready, 1)
            flat = lambda a: a.rearrange("p e t -> p (e t)")
            dve.wait_ge(rank_done, 1)
            then(V.tensor_tensor_scan(flat(incl[:, :, :]), seg[:, :], tot_ps, 0.0, ALU.mult, ALU.add))
            then(V.tensor_tensor(flat(base[:, :, :]), flat(incl[:, :, :]), tot_ps, ALU.subtract))
            V.tensor_tensor(pos[:, :, :], base[:, :, :], rank_ps, ALU.add).then_inc(pos_ready, 1)
            dve.wait_ge(pos_ready, 1)
            then(V.tensor_scalar(over[:, :, :], pos[:, :, :], float(CAP), float(2 * ZROW), ALU.is_ge, ALU.mult))
            then(V.tensor_tensor(base[:, :, :], pos[:, :, :], over[:, :, :], ALU.add))
            then(V.tensor_tensor(slot[:, :, :], base[:, :, :],
                                 slot0[:, :].rearrange("p (e o) -> p e o", o=1).to_broadcast([P, E, NT]),
                                 ALU.add))
            V.tensor_tensor(pick[:, 0, :, :], oh1[:, :, :], slot[:, :, :].rearrange("p e t -> p t e"), ALU.mult)
            then(V.tensor_tensor(pick[:, 1, :, :], oh2[:, :, :], slot[:, :, :].rearrange("p e t -> p t e"),
                                 ALU.mult))
            then(V.tensor_reduce(slot_f[:, :, :], pick[:, :, :, :], AX_X, ALU.add))
            V.tensor_scalar(slot_i[:, :, :], slot_f[:, :, :], float(ZROW), None, ALU.min
                            ).then_inc(slots_ready, 1)
            dve.wait_ge(e2_ready, 1)
            then(V.tensor_scalar(e2p[:, :], e2[:, :], 1.0, None, ALU.add))
            then(V.reciprocal(wgt[:, 0, :], e2p[:, :]))
            then(V.tensor_tensor(wgt[:, 1, :], wgt[:, 0, :], e2[:, :], ALU.mult))

            dve.wait_ge(sw_hi_s, 1)
            V.tensor_tensor(sw_lo[:, :, :], sw_raw[:, :, :], sw_hi[:, :, :].bitcast(F32), ALU.subtract
                            ).then_inc(sw_ready, 1)
            for b in range(B):
                for h in range(2):
                    dve.wait_ge(att_done, 2 * b + h + 1)
                    o = down_b[h][:, 0:2 * (D + 1)].rearrange("p (r c) -> p r c", r=2)
                    t = TG * b + 2 * h
                    then(V.reciprocal(rden[:, t:t + 2], o[:, :, D]))
                    for r in range(2):
                        last = V.scalar_tensor_tensor(out=acc[:, t + r, :], in0=o[:, r, 0:D],
                                                      scalar=rden[:, t + r:t + r + 1], in1=acc[:, t + r, :],
                                                      op0=ALU.mult, op1=ALU.add)
                    last.then_inc(att_added, 1)

            def mult_chunk(q, n, hid):
                dve.wait_ge(silu_ready, q + 1)
                V.tensor_tensor(hid, up_b[q % 2][:, 0:n], silu[:, q % 2, 0:n], ALU.mult).then_inc(hid_ready, 1)

            def split_weights(e):
                dve.wait_ge(ew_hi_s, e + 1)
                V.tensor_tensor(ew_lo[:, e % 2, :, :], ew_raw[:, e % 2, :, :],
                                ew_hi[:, e % 2, :, :].bitcast(F32), ALU.subtract).then_inc(ew_ready, 1)

            def slots_lo(e):
                dve.wait_ge(xg_hi_s, e + 1)
                V.tensor_tensor(xgT_lo[:, e % 2, :], turn_b[e % 2][:, 0:CAP],
                                xgT_hi[:, e % 2, :].bitcast(F32), ALU.subtract).then_inc(xg_ready, 1)

            def block_sum(b):
                dve.wait_ge(job_done, block_job(b) + 1)
                dve.wait_ge(att_added, 2 * (b + 1))
                a = acc[:, TG * b:TG * b + TG, :].rearrange("p t d -> p (t d)")
                V.tensor_tensor(a, down_b[block_job(b) % 2][:, :], a, ALU.add).then_inc(block_added, 1)

            def mult_block(b, between):
                if b >= 2:
                    dve.wait_ge(job_done, block_job(b - 2) + 1)
                for c in range(CS):
                    mult_chunk(block_chunk(b) + c, S, hid_s[:, b % 2, c, :])
                    between(c)

            for b in range(EARLY):
                def between(c, b=b):
                    if b == EARLY - 1 and c == CS // 2:
                        split_weights(0)
                mult_block(b, between)
            block_sum(0)
            slots_lo(0)
            for e in range(E):
                if e + 1 < E:
                    slots_lo(e + 1)
                if e >= 2:
                    dve.wait_ge(job_done, expert_job(e - 2) + 1)
                for c in range(CR):
                    mult_chunk(expert_chunk(e) + c, CAP, hid_e[:, e % 2, c, :])
                    if c == 0 and e + 1 < E:
                        split_weights(e + 1)
                if e == 0:
                    block_sum(1)
            for b in range(EARLY, B):
                mult_block(b, lambda c: None)
                if b > EARLY:
                    block_sum(b - 1)
            block_sum(B - 1)
            for t in range(NT):
                dve.wait_ge(block_added, t // TG + 1)
                dve.wait_ge(gathered[t], 32)
                then(V.scalar_tensor_tensor(out=acc[:, t, :], in0=got[:, t, 0, :], scalar=wgt[:, 0, t:t + 1],
                                            in1=acc[:, t, :], op0=ALU.mult, op1=ALU.add))
                V.scalar_tensor_tensor(out=acc[:, t, :], in0=got[:, t, 1, :], scalar=wgt[:, 1, t:t + 1],
                                       in1=acc[:, t, :], op0=ALU.mult, op1=ALU.add).then_inc(summed, 1)

        @block.tensor
        def _(pe):
            M = nc.tensor.matmul

            def parts(o, w_hi, w_lo, m_hi, m_lo):
                M(o, w_hi, m_hi, start=True, stop=False)
                M(o, w_hi, m_lo, start=False, stop=False)
                return M(o, w_lo, m_hi, start=False, stop=True)

            pe.wait_ge(consts, 1)
            pe.wait_ge(rw_loaded, 16)
            nc.tensor.transpose(rw_ps, rw_raw[:, :], ident[0:E, 0:E]).then_inc(rwT_turned, 1)

            def turn(g):
                pe.wait_ge(xn_ready, g + 1)
                if g >= 2:
                    pe.wait_ge(xnT_ready, g - 1)
                for j in range(TG):
                    last = nc.tensor.transpose(turn_b[g % 2][:, P * j:P * j + P], xn[:, TG * g + j, 0:D],
                                               ident[:, :])
                last.then_inc(xnT_turned, 1)

            def project(g):
                cols = slice(S * g, S * g + S)
                pe.wait_ge(xnT_ready, g + 1)
                if g == 0:
                    pe.wait_ge(rwT_ready, 1)
                    pe.wait_ge(U_ready, 1)
                last = parts(bank[g][0:3 * R, :], U_hi[:, :, :].rearrange("p j r -> p (j r)"),
                             U_lo[:, :, :].rearrange("p j r -> p (j r)"), xnT_hi[:, cols], xnT_lo[:, cols])
                last.then_inc(y_done, 1)
                for t in range(TG * g, TG * g + TG):
                    M(lg_ps[:, t, :], xnT_hi[:, P * t:P * t + P], rwT[:, :], start=True, stop=False)
                    last = M(lg_ps[:, t, :], xnT_lo[:, P * t:P * t + P], rwT[:, :], start=False, stop=True)
                last.then_inc(lg_done, 1)

            turn(0)
            for g in range(1, B):
                turn(g)
                project(g - 1)
            project(B - 1)
            pe.wait_ge(dve_const, 1)
            for g in range(B):
                cols = slice(S * g, S * g + S)
                pe.wait_ge(ysq_ready, g + 1)
                for t in range(TG * g, TG * g + TG):
                    M(nb_ps[:, 2 * t:2 * t + 2], ysq[:, P * t:P * t + P], half[:, :], start=True, stop=True)
                M(bank[g][3 * R:3 * R + 2, :], half[:, :], ysq[:, cols], start=True, stop=True
                  ).then_inc(n_done, 1)

            def scores(b):
                pe.wait_ge(y_ready, B)
                for j in range(TG):
                    if b >= 1:
                        pe.wait_ge(prob_ready, TG * (b - 1) + j + 1)
                    M(bank[j][:, :], yL[0:3 * R + 2, S * b + P * j:S * b + P * j + P],
                      yR[0:3 * R + 2, S * b:S * b + S], start=True, stop=True).then_inc(score_done, 1)

            def attend(b):
                pe.wait_ge(prob_ready, TG * (b + 1))
                if b == 0:
                    pe.wait_ge(nb_copied, 1)
                    pe.wait_ge(lg_copied, 1)
                for i in range(TG):
                    if b >= 1 and i % 2 == 0:
                        pe.wait_ge(att_added, 2 * (b - 1) + i // 2 + 1)
                    for j in range(TG):
                        last = M(down_b[i // 2][:, (D + 1) * (i % 2):(D + 1) * (i % 2 + 1)],
                                 probs[:, b % 2, j, P * i:P * i + P], xn[:, TG * b + j, :],
                                 start=(j == 0), stop=(j == TG - 1))
                    if i % 2 == 1:
                        last.then_inc(att_done, 1)

            def ranks():
                pe.wait_ge(sel_ready, 1)
                s = sel[:, :, :].rearrange("p e t -> p (e t)")
                M(bank[6][:, 0:E * NT], tri[:, :], s, start=True, stop=True)
                M(tot_ps, ones_bf[:, :], s, start=True, stop=True).then_inc(rank_done, 1)

            scores(0)
            scores(1)
            attend(0)
            ranks()
            for b in range(1, B):
                if b + 1 < B:
                    scores(b + 1)
                attend(b)

            def up_chunk(q, n, w_hi, w_lo, m_hi, m_lo):
                if q >= 2:
                    pe.wait_ge(hid_ready, q - 1)
                parts(gate_b[q % 2][:, 0:n], w_hi(0), w_lo(0), m_hi, m_lo)
                parts(up_b[q % 2][:, 0:n], w_hi(1), w_lo(1), m_hi, m_lo).then_inc(chunk_done, 1)

            def up_block(b, cs=range(CS)):
                if b == 0:
                    pe.wait_ge(sw_ready, 1)
                for c in cs:
                    up_chunk(block_chunk(b) + c, S, lambda w: sw_hi[:, w, P * c:P * c + P],
                             lambda w: sw_lo[:, w, P * c:P * c + P],
                             xnT_hi[:, S * b:S * b + S], xnT_lo[:, S * b:S * b + S])

            def bank_free(job):
                if job < 2:
                    pe.wait_ge(att_added, 2 * B)
                elif job - 2 < EARLY:
                    pe.wait_ge(block_added, job - 1)
                elif job - 2 < EARLY + E:
                    pe.wait_ge(eo_ready, job - 2 - EARLY + 1)

            def down_block(b):
                job = block_job(b)
                bank_free(job)
                if b == 0:
                    pe.wait_ge(sd_loaded, 16)
                pe.wait_ge(hid_ready, block_chunk(b) + CS)
                for i in range(TG):
                    for c in range(CS):
                        last = M(down_b[job % 2][:, D * i:D * i + D], hid_s[:, b % 2, c, P * i:P * i + P],
                                 sd[:, c, :], start=(c == 0), stop=(c == CS - 1))
                last.then_inc(job_done, 1)

            def turn_slots(e):
                s = e % 2
                pe.wait_ge(xg_loaded[s], 32 * (e // 2 + 1))
                if e >= 2:
                    pe.wait_ge(xg_ready, e - 1)
                else:
                    pe.wait_ge(pos_ready, 1)
                for r in range(3):
                    n = P if r < 2 else TAIL
                    last = nc.tensor.transpose(turn_b[s][:, P * r:P * r + n], xg[0:n, s, r, :],
                                               ident[0:n, 0:n])
                last.then_inc(xg_turned, 1)

            def up_expert(e):
                s = e % 2
                pe.wait_ge(ew_ready, e + 1)
                pe.wait_ge(xg_ready, e + 1)
                for c in range(CR):
                    up_chunk(expert_chunk(e) + c, CAP, lambda w: ew_hi[:, s, w, P * c:P * c + P],
                             lambda w: ew_lo[:, s, w, P * c:P * c + P], xgT_hi[:, s, :], xgT_lo[:, s, :])

            def down_expert(e):
                job = expert_job(e)
                bank_free(job)
                pe.wait_ge(rd_loaded[e % 3], 16 * (e // 3 + 1))
                pe.wait_ge(hid_ready, expert_chunk(e) + CR)
                for r in range(3):
                    n = P if r < 2 else TAIL
                    for c in range(CR):
                        last = M(down_b[job % 2][0:n, D * r:D * r + D], hid_e[:, e % 2, c, P * r:P * r + n],
                                 rd[:, e % 3, c, :], start=(c == 0), stop=(c == CR - 1))
                last.then_inc(job_done, 1)

            up_block(0)
            up_block(1)
            down_block(0)
            turn_slots(0)
            for e in range(E):
                if e + 1 < E:
                    turn_slots(e + 1)
                up_expert(e)
                if e == 0:
                    down_block(1)
                else:
                    down_expert(e - 1)
            up_block(2, range(0, 2))
            down_expert(E - 1)
            up_block(2, range(2, CS))
            up_block(3)
            down_block(2)
            down_block(3)


_INS = ['L0_attn_x', 'L0_attn_U', 'L0_ffn_router_w', 'L0_ffn_rg', 'L0_ffn_ru', 'L0_ffn_rd',
        'L0_ffn_sg', 'L0_ffn_su', 'L0_ffn_sd']
_OUTS = [((4, 512, 128), 'float32')]


def kernel(**inputs):
    import numpy as _np
    import concourse.bacc as _bacc
    from concourse import mybir as _mybir
    from concourse.bass_utils import run_bass_kernel_spmd as _run

    nc = _bacc.Bacc("TRN2", target_bir_lowering=False, num_devices=1)
    arrays, args = {}, []
    for name in _INS:
        a = _np.ascontiguousarray(inputs[name])
        arrays[f"in_{name}_dram"] = a
        args.append(nc.dram_tensor(f"in_{name}_dram", a.shape, _mybir.dt.from_np(a.dtype), kind="ExternalInput").ap())
    for i, (shape, dtype) in enumerate(_OUTS):
        dt = _mybir.dt.from_np(_np.dtype(dtype))
        args.append(nc.dram_tensor(f"out_{i}_dram", shape, dt, kind="ExternalOutput").ap())
    moe_attention_kernel(nc, *args)
    r = _run(nc, [arrays], core_ids=[0])
    got = tuple(r.results[0][f"out_{i}_dram"] for i in range(len(_OUTS)))
    return got[0]
```

```python
from contextlib import ExitStack

import concourse.bass as bass
from concourse import mybir

ALU = mybir.AluOpType
ACT = mybir.ActivationFunctionType
AX_X = mybir.AxisListType.X
F32 = mybir.dt.float32
F32R = mybir.dt.float32r
BF16 = mybir.dt.bfloat16
I32 = mybir.dt.int32

P = 128
LN_EPS = 1e-5
RMS_EPS = 1.1920928955078125e-07
CAP_FACTOR = 1.25
TOP_K = 2


def moe_attention_kernel(nc, x_in, U_in, rw_in, rg_in, ru_in, rd_in, sg_in, su_in, sd_in, out):
    B, S, D = x_in.shape
    R = U_in.shape[1]
    E, _, IR = rg_in.shape
    IS = sg_in.shape[1]
    assert D == P and S == 512 and R == 32 and TOP_K == 2
    T = B * S
    NT = T // P
    TG = S // P
    CAP = max(int(CAP_FACTOR * T / E), 1)
    CR = IR // P
    CS = IS // P
    ZROW = E * CAP
    TAIL = CAP - 2 * P
    assert 0 < TAIL <= P and E <= 8
    EARLY = 2
    ZCH = E * CAP // P

    def block_job(b):
        return b if b == 0 else b + E

    def block_chunk(b):
        return CS * b if b < EARLY else CS * b + CR * E

    def expert_job(e):
        return 1 + e

    def expert_chunk(e):
        return CS * EARLY + CR * e

    slots_dram = nc.dram_tensor("slots_dram", (E * CAP, D), F32).ap()
    eout_dram = nc.dram_tensor("eout_dram", (E * CAP + 1, D), F32).ap()

    x_v = x_in.rearrange("b (t p) d -> b p t d", p=P)
    out_v = out.rearrange("b (t p) d -> b p t d", p=P)

    def slot_rows(dram, e):
        lo = e * CAP
        return (dram[lo:lo + 2 * P, :].rearrange("(p r) d -> p r d", r=2),
                dram[lo + 2 * P:lo + CAP, :])

    with ExitStack() as ctx:
        def sb(name, shape, dt=F32):
            return ctx.enter_context(nc.sbuf_tensor(name, shape, dt))

        def sem(name):
            return ctx.enter_context(nc.semaphore(name))

        acc = sb("acc", [P, NT, D])
        xn = sb("xn", [P, NT, D + 1])
        xnT_hi = sb("xnT_hi", [P, T], F32R)
        xnT_lo = sb("xnT_lo", [P, T], F32R)
        ident = sb("ident", [P, P])
        zeros = sb("zeros", [P, D])
        minus_ones = sb("minus_ones", [P, P])
        tri = sb("tri", [P, P], BF16)
        ones_bf = sb("ones_bf", [P, P], BF16)
        ones_f = sb("ones_f", [P, P])
        e_ids = sb("e_ids", [P, E])
        e_ids_i = sb("e_ids_i", [P, E], I32)
        part_i = sb("part_i", [P, 1], I32)
        row97 = sb("row97", [P, 1])
        seg = sb("seg", [P, E * NT])
        slot0_i = sb("slot0_i", [P, E, NT], I32)
        slot0 = sb("slot0", [P, E, NT])
        slot_end = sb("slot_end", [P, E, NT])
        half = sb("half", [R, 2])
        rw_raw = sb("rw_raw", [E, D])
        rwT = sb("rwT", [P, 2 * E], F32R)
        U_raw = sb("U_raw", [P, R])
        U_hi = sb("U_hi", [P, 3, R], F32R)
        U_lo = sb("U_lo", [P, 3, R], F32R)
        yL = sb("yL", [P, T], F32R)
        yR = sb("yR", [P, T], F32R)
        ysq = sb("ysq", [R, T])
        nhi = sb("nhi", [P, S], F32R)
        nbias = sb("nbias", [P, NT])
        rden = sb("rden", [P, NT])
        stats = sb("stats", [P, NT, 6])
        mv = sb("mv", [P, NT, 2])
        ve = sb("ve", [P, 2, NT])
        root = sb("root", [P, 2, NT])
        nw_a = sb("nw_a", [P, 2, NT])
        nw_b = sb("nw_b", [P, 2, NT])
        nw_c = sb("nw_c", [P, 2, NT])
        rstd = sb("rstd", [P, 2, NT])
        nmr = sb("nmr", [P, NT])
        std = sb("std", [P, NT])
        rms = sb("rms", [P, NT])
        lg = sb("lg", [P, NT, 2 * E])
        z = sb("z", [P, NT, E])
        z2 = sb("z2", [P, NT, E])
        key = sb("key", [P, NT, E])
        chosen = sb("chosen", [P, 2, NT, E])
        sel = sb("sel", [P, E, NT], BF16)
        m1 = sb("m1", [P, NT])
        m2 = sb("m2", [P, NT])
        i1 = sb("i1", [P, NT])
        i2 = sb("i2", [P, NT])
        e2 = sb("e2", [P, NT])
        e2p = sb("e2p", [P, NT])
        wgt = sb("wgt", [P, 2, NT])
        incl = sb("incl", [P, E, NT])
        pos = sb("pos", [P, E, NT])
        over = sb("over", [P, E, NT])
        slot = sb("slot", [P, E, NT])
        pick = sb("pick", [P, 2, NT, E])
        slot_f = sb("slot_f", [P, 2, NT])
        slot_i = sb("slot_i", [P, 2, NT], I32)
        sw_raw = sb("sw_raw", [P, 2, IS])
        sw_hi = sb("sw_hi", [P, 2, IS], F32R)
        sw_lo = sb("sw_lo", [P, 2, IS], F32R)
        sd = sb("sd", [P, CS, D])
        ew_raw = sb("ew_raw", [P, 2, 2, IR])
        ew_hi = sb("ew_hi", [P, 2, 2, IR], F32R)
        ew_lo = sb("ew_lo", [P, 2, 2, IR], F32R)
        rd = sb("rd", [P, 3, CR, D])
        xg = sb("xg", [P, 2, 3, D])
        xgT_hi = sb("xgT_hi", [P, 2, CAP], F32R)
        xgT_lo = sb("xgT_lo", [P, 2, CAP], F32R)
        silu = sb("silu", [P, 2, S])
        hid_s = sb("hid_s", [P, 2, CS, S])
        assert CS == 2 * TG and B >= 2
        probs = hid_s[:, 1, :, :].rearrange("p (b j) i -> p b j i", b=2)
        hid_e = sb("hid_e", [P, 2, CR, CAP])
        eo = sb("eo", [P, 2, 3, D])
        got = sb("got", [P, NT, 2, D])

        bank = [ctx.enter_context(nc.psum_tensor(f"bank{i}", [P, 512], F32)) for i in range(8)]
        gate_b = [bank[0], bank[2]]
        up_b = [bank[1], bank[3]]
        down_b = [bank[4], bank[5]]
        turn_b = [bank[6], bank[7]]
        nb_ps = bank[TG - 1][:, 0:2 * TG].rearrange("p (t c) -> p t c", c=2)
        rw_ps = bank[4][:, 64:64 + E]
        lg_ps = bank[5][:, 0:NT * 2 * E].rearrange("p (t c) -> p t c", t=NT)
        rank_cols = slice(NT * 2 * E, NT * 3 * E)
        rank_ps = bank[5][:, rank_cols].rearrange("p (e t) -> p e t", e=E)
        tot_ps = bank[5][:, NT * 3 * E:NT * 4 * E]

        x_in_s = [sem(f"x_loaded{g}") for g in range(B)]
        rw_loaded, U_loaded = sem("rw_loaded"), sem("U_loaded")
        sw_loaded = [sem(f"sw_loaded{h}") for h in range(2)]
        sd_loaded = sem("sd_loaded")
        ew_loaded = [sem(f"ew_loaded{i}") for i in range(2)]
        rd_loaded = [sem(f"rd_loaded{i}") for i in range(3)]
        xg_loaded = [sem(f"xg_loaded{i}") for i in range(2)]
        zero_filled = sem("zero_filled")
        scattered = sem("scattered")
        eo_written = [sem(f"eo_written{i}") for i in range(2)]
        eo_last_written = sem("eo_last_written")
        gathered = [sem(f"gathered{t}") for t in range(NT)]
        out_written = sem("out_written")
        pool_step = sem("pool_step")
        consts = sem("consts")
        zeros_set = sem("zeros_set")
        dve_const = sem("dve_const")
        dve_step = sem("dve_step")
        ve_ready = sem("ve_ready")
        root_ready = sem("root_ready")
        rstd_ready, nmr_ready = sem("rstd_ready"), sem("nmr_ready")
        xn_ready = sem("xn_ready")
        xn_ready_act = sem("xn_ready_act")
        rwT_turned, rwT_hi_s, rwT_ready = sem("rwT_turned"), sem("rwT_hi_s"), sem("rwT_ready")
        U_hi_s, U_ready = sem("U_hi_s"), sem("U_ready")
        xnT_turned, xnT_hi_s, xnT_ready = sem("xnT_turned"), sem("xnT_hi_s"), sem("xnT_ready")
        lg_done, lg_copied = sem("lg_done"), sem("lg_copied")
        y_done, y_hi_s, y_ready = sem("y_done"), sem("y_hi_s"), sem("y_ready")
        ysq_ready, n_done, nhi_ready = sem("ysq_ready"), sem("n_done"), sem("nhi_ready")
        nb_done, nb_copied = sem("nb_done"), sem("nb_copied")
        e2_asked, e2_ready = sem("e2_asked"), sem("e2_ready")
        sel_ready, rank_done = sem("sel_ready"), sem("rank_done")
        pos_ready = sem("pos_ready")
        slots_ready = sem("slots_ready")
        score_done, prob_ready = sem("score_done"), sem("prob_ready")
        att_done, att_added = sem("att_done"), sem("att_added")
        sw_hi_s, sw_ready = sem("sw_hi_s"), sem("sw_ready")
        ew_hi_s, ew_ready = sem("ew_hi_s"), sem("ew_ready")
        xg_turned, xg_hi_s, xg_ready = sem("xg_turned"), sem("xg_hi_s"), sem("xg_ready")
        chunk_done, silu_ready, hid_ready = sem("chunk_done"), sem("silu_ready"), sem("hid_ready")
        job_done = sem("job_done")
        block_added, eo_ready = sem("block_added"), sem("eo_ready")
        summed = sem("summed")

        block = ctx.enter_context(nc.Block())

        @block.sync
        def _(sp):
            def load_expert_weights(e, s):
                sp.dma_start(ew_raw[:, s, 0, :], rg_in[e]).then_inc(ew_loaded[s], 16)
                sp.dma_start(ew_raw[:, s, 1, :], ru_in[e]).then_inc(ew_loaded[s], 16)

            def load_down(e, s):
                sp.dma_start(rd[:, s, :, :], rd_in[e].rearrange("(c p) d -> p c d", p=P)
                             ).then_inc(rd_loaded[s], 16)

            def load_slots(e, s):
                main, tail = slot_rows(slots_dram, e)
                sp.dma_start(xg[:, s, 0:2, :], main).then_inc(xg_loaded[s], 16)
                sp.dma_start(xg[0:TAIL, s, 2, :], tail).then_inc(xg_loaded[s], 16)

            sp.dma_start(acc[:, 0:TG, :], x_v[0]).then_inc(x_in_s[0], 16)
            sp.dma_start(rw_raw[:, :], rw_in).then_inc(rw_loaded, 16)
            sp.dma_start(U_raw[:, :], U_in).then_inc(U_loaded, 16)
            for g in range(1, B):
                sp.dma_start(acc[:, TG * g:TG * g + TG, :], x_v[g]).then_inc(x_in_s[g], 16)
            for h in range(2):
                cols = slice(IS // 2 * h, IS // 2 * (h + 1))
                sp.dma_start(sw_raw[:, 0, cols], sg_in[:, cols]).then_inc(sw_loaded[h], 16)
                sp.dma_start(sw_raw[:, 1, cols], su_in[:, cols]).then_inc(sw_loaded[h], 16)
            sp.wait_ge(zeros_set, 1)
            sp.dma_start(slots_dram.rearrange("(p a) d -> p a d", p=P),
                         zeros[:, :].rearrange("p (o d) -> p o d", o=1).to_broadcast([P, ZCH, D])
                         ).then_inc(zero_filled, 16)
            sp.dma_start(eout_dram[ZROW:ZROW + 1, :], zeros[0:1, 0:D]).then_inc(zero_filled, 16)
            sp.dma_start(sd[:, :, :], sd_in.rearrange("(c p) d -> p c d", p=P)).then_inc(sd_loaded, 16)
            for e in range(2):
                load_expert_weights(e, e)
                load_down(e, e)
            sp.wait_ge(scattered, 16 * 2 * NT)
            for e in range(2):
                load_slots(e, e)
            for e in range(E - 2):
                sp.wait_ge(ew_ready, e + 1)
                load_expert_weights(e + 2, e % 2)
                sp.wait_ge(xg_turned, e + 1)
                load_slots(e + 2, e % 2)
                if e >= 1:
                    sp.wait_ge(job_done, expert_job(e - 1) + 1)
                load_down(e + 2, (e + 2) % 3)
            sp.wait_ge(eo_ready, E)
            main, tail = slot_rows(eout_dram, E - 1)
            sp.dma_start(main, eo[:, (E - 1) % 2, 0:2, :]).then_inc(eo_last_written, 16)
            sp.dma_start(tail, eo[0:TAIL, (E - 1) % 2, 2, :]).then_inc(eo_last_written, 16)
            for g in range(B - 1):
                sp.wait_ge(summed, TG * (g + 1))
                sp.dma_start(out_v[g], acc[:, TG * g:TG * g + TG, :]).then_inc(out_written, 16)
            sp.wait_ge(block_added, B)
            sp.dma_start(out_v[B - 1], acc[:, TG * (B - 1):NT, :]).then_inc(out_written, 16)
            sp.wait_ge(out_written, 16 * B)

        @block.gpsimd
        def _(pool):
            steps = [0]

            def after(ins):
                steps[0] += 1
                ins.then_inc(pool_step, 1)
                pool.wait_ge(pool_step, steps[0])

            G = nc.gpsimd
            G.memset(minus_ones[:, :], -1.0)
            after(G.memset(ones_f[:, :], 1.0))
            G.affine_select(out=ident[:, :], in_=ones_f[:, :], compare_op=ALU.is_equal,
                            fill=0.0, base=0, pattern=[[-1, P]], channel_multiplier=1)
            G.affine_select(out=tri[:, :], in_=minus_ones[:, :], compare_op=ALU.is_ge,
                            fill=0.0, base=0, pattern=[[-1, P]], channel_multiplier=1)
            G.iota(slot0_i[:, :, :], pattern=[[CAP, E], [0, NT]], base=0, channel_multiplier=0)
            G.iota(e_ids_i[:, :], pattern=[[1, E]], base=0, channel_multiplier=0)
            G.iota(part_i[:, :], pattern=[[0, 1]], base=0, channel_multiplier=1)
            G.affine_select(out=seg[:, :].rearrange("p (e t) -> p e t", e=E),
                            in_=ones_f[:, 0:E * NT].rearrange("p (e t) -> p e t", e=E),
                            compare_op=ALU.is_gt, fill=0.0, base=0,
                            pattern=[[0, E], [1, NT]], channel_multiplier=0).then_inc(consts, 1)
            pool.wait_ge(consts, 1)
            after(G.memset(yL[3 * R:3 * R + 2, :].bitcast(F32), 1.0))
            pool.wait_ge(U_hi_s, 1)
            for j in range(3):
                last = G.tensor_tensor(U_lo[:, j, :], U_raw[:, :], U_hi[:, j, :].bitcast(F32), ALU.subtract)
            last.then_inc(U_ready, 1)
            for i in range(CS // 2):
                cols = slice(2 * P * i, 2 * P * (i + 1))
                pool.wait_ge(sw_hi_s, i + 1)
                G.tensor_tensor(sw_lo[:, :, cols], sw_raw[:, :, cols], sw_hi[:, :, cols].bitcast(F32),
                                ALU.subtract).then_inc(sw_ready, 1)
            pool.wait_ge(zero_filled, 32)
            pool.wait_ge(xn_ready, B)
            pool.wait_ge(xn_ready_act, B)
            pool.wait_ge(slots_ready, 1)
            for t in range(NT):
                for k in range(2):
                    G.indirect_dma_start(
                        slots_dram, bass.IndirectOffsetOnAxis(slot_i[:, k, t:t + 1], 0), xn[:, t, 0:D], None,
                        bounds_check=E * CAP - 1, oob_is_err=False).then_inc(scattered, 16)

            def split_weights(e):
                pool.wait_ge(ew_hi_s, 2 * (e + 1))
                G.tensor_tensor(ew_lo[:, e % 2, :, :], ew_raw[:, e % 2, :, :],
                                ew_hi[:, e % 2, :, :].bitcast(F32), ALU.subtract).then_inc(ew_ready, 1)

            split_weights(0)
            for e in range(E):
                if e + 1 < E:
                    split_weights(e + 1)
                if e >= 1:
                    main, tail = slot_rows(eout_dram, e - 1)
                    pool.wait_ge(eo_ready, e)
                    s = (e - 1) % 2
                    G.dma_start(main, eo[:, s, 0:2, :]).then_inc(eo_written[s], 16)
                    G.dma_start(tail, eo[0:TAIL, s, 2, :]).then_inc(eo_written[s], 16)
            for s in range(2):
                pool.wait_ge(eo_written[s], 32 * ((E - s) // 2))
            pool.wait_ge(eo_last_written, 32)
            for t in range(NT):
                for k in range(2):
                    G.indirect_dma_start(
                        got[:, t, k, :], None, eout_dram, bass.IndirectOffsetOnAxis(slot_i[:, k, t:t + 1], 0),
                        bounds_check=ZROW, oob_is_err=False).then_inc(gathered[t], 16)

        @block.scalar
        def _(act):
            C = nc.scalar

            def root_of(gs):
                ts = slice(TG * gs[0], TG * (gs[-1] + 1))
                act.wait_ge(ve_ready, gs[0] // 2 + 1)
                C.activation(root[:, :, ts], ve[:, :, ts], ACT.Sqrt, scale=0.25).then_inc(root_ready, 1)

            def normalize(g):
                act.wait_ge(nmr_ready, g // 2 + 1)
                for t in range(TG * g + TG // 2, TG * g + TG):
                    last = C.activation(xn[:, t, 0:D], acc[:, t, :], ACT.Identity, bias=nmr[:, t:t + 1],
                                        scale=rstd[:, 0, t:t + 1])
                last.then_inc(xn_ready_act, 1)

            def turned_hi(g):
                act.wait_ge(xnT_turned, g + 1)
                C.copy(xnT_hi[:, S * g:S * g + S], turn_b[g % 2][:, :]).then_inc(xnT_hi_s, 1)

            def y_hi(g):
                cols = slice(S * g, S * g + S)
                act.wait_ge(y_done, g + 1)
                C.copy(yL[0:3 * R, cols], turn_b[g % 2][0:3 * R, :])
                C.copy(yR[0:3 * R, cols], turn_b[g % 2][0:3 * R, :]).then_inc(y_hi_s, 1)
                C.activation(ysq[:, cols], turn_b[g % 2][0:R, :], ACT.Square).then_inc(ysq_ready, 1)

            def n_hi(g):
                act.wait_ge(n_done, g + 1)
                if g > 0:
                    act.wait_ge(y_ready, g)
                C.copy(nhi[3 * R:3 * R + 2, :], turn_b[g % 2][3 * R:3 * R + 2, :]).then_inc(nhi_ready, 1)

            def exps(b):
                act.wait_ge(nb_done, b + 1)
                C.mul(nbias[:, TG * b:TG * b + TG], nb_ps[:, :, 0], 2.0).then_inc(nb_copied, 1)
                for j in range(TG):
                    t = TG * b + j
                    act.wait_ge(score_done, t + 1)
                    if j == 0:
                        act.wait_ge(nb_copied, b + 1)
                        if b >= 2:
                            act.wait_ge(att_done, 2 * (b - 1))
                    C.activation(probs[:, b % 2, j, :], bank[j][:, :], ACT.Exp,
                                 bias=nbias[:, t:t + 1], scale=2.0).then_inc(prob_ready, 1)

            def silu_chunk(q, n):
                act.wait_ge(chunk_done, q + 1)
                if q >= 2:
                    act.wait_ge(hid_ready, q - 1)
                C.activation(silu[:, q % 2, 0:n], gate_b[q % 2][:, 0:n], ACT.Silu).then_inc(silu_ready, 1)

            def round_weights(e, w):
                if w == 0:
                    act.wait_ge(ew_loaded[e % 2], 32 * (e // 2 + 1))
                    if e >= 2:
                        act.wait_ge(chunk_done, expert_chunk(e - 1))
                C.copy(ew_hi[:, e % 2, w, :], ew_raw[:, e % 2, w, :]).then_inc(ew_hi_s, 1)

            def slots_hi(e):
                act.wait_ge(xg_turned, e + 1)
                if e >= 2:
                    act.wait_ge(chunk_done, expert_chunk(e - 1))
                C.copy(xgT_hi[:, e % 2, :], turn_b[e % 2][:, 0:CAP]).then_inc(xg_hi_s, 1)

            def expert_out(e):
                act.wait_ge(job_done, expert_job(e) + 1)
                if e >= 2:
                    act.wait_ge(eo_written[e % 2], 32 * (e // 2))
                o = down_b[expert_job(e) % 2]
                C.copy(eo[:, e % 2, 0:2, :], o[:, 0:2 * D].rearrange("p (r d) -> p r d", r=2))
                C.copy(eo[0:TAIL, e % 2, 2, :], o[0:TAIL, 2 * D:3 * D]).then_inc(eo_ready, 1)

            act.wait_ge(U_loaded, 16)
            for j in range(3):
                last = C.copy(U_hi[:, j, :], U_raw[:, :])
            last.then_inc(U_hi_s, 1)
            act.wait_ge(rwT_turned, 1)
            C.copy(rwT[:, 0:E], rw_ps).then_inc(rwT_hi_s, 1)
            def round_shared(i):
                cols = slice(2 * P * i, 2 * P * (i + 1))
                act.wait_ge(sw_loaded[2 * i * P // (IS // 2)], 32)
                C.copy(sw_hi[:, :, cols], sw_raw[:, :, cols]).then_inc(sw_hi_s, 1)

            root_of((0, 1))
            normalize(0)
            normalize(1)
            turned_hi(0)
            round_shared(0)
            root_of((2, 3))
            turned_hi(1)
            normalize(2)
            normalize(3)
            round_shared(1)
            turned_hi(2)
            turned_hi(B - 1)
            for i in range(B - 2, CS // 2):
                round_shared(i)
                if i == B - 2:
                    act.wait_ge(lg_done, B)
                    C.copy(lg[:, :, :], lg_ps).then_inc(lg_copied, 1)
            for c in range(CS):
                silu_chunk(c, S)
                if c == 1:
                    y_hi(0)
                if c == 3:
                    y_hi(1)
                if c == 4:
                    n_hi(0)
            act.wait_ge(e2_asked, 1)
            C.activation(e2[:, :], m2[:, :], ACT.Exp).then_inc(e2_ready, 1)
            exps(0)
            n_hi(1)
            y_hi(2)
            n_hi(2)
            y_hi(3)
            exps(1)
            n_hi(3)
            exps(2)
            round_weights(0, 0)
            round_weights(0, 1)
            exps(3)
            for c in range(CS):
                silu_chunk(block_chunk(1) + c, S)
            slots_hi(0)
            for e in range(E):
                if e + 1 < E:
                    slots_hi(e + 1)
                for c in range(CR):
                    silu_chunk(expert_chunk(e) + c, CAP)
                    if c < 2 and e + 1 < E:
                        round_weights(e + 1, c)
                if e >= 1:
                    expert_out(e - 1)
            expert_out(E - 1)
            for b in range(EARLY, B):
                for c in range(CS):
                    silu_chunk(block_chunk(b) + c, S)

        @block.vector
        def _(dve):
            steps = [0]
            V = nc.vector

            def mark(ins):
                steps[0] += 1
                ins.then_inc(dve_step, 1)

            def settle():
                dve.wait_ge(dve_step, steps[0])

            def then(ins):
                mark(ins)
                settle()

            V.memset(zeros[:, :], 0.0).then_inc(zeros_set, 1)
            V.memset(half[:, :], -0.5)
            V.memset(ones_bf[:, :], 1.0)
            V.memset(xn[:, :, D:D + 1], 1.0)
            dve.wait_ge(consts, 1)
            V.tensor_copy(e_ids[:, :], e_ids_i[:, :])
            then(V.tensor_scalar(row97[:, :], part_i[:, :], float(3 * R + 1), -1.0, ALU.is_equal, ALU.mult))
            then(V.tensor_copy(slot0[:, :, :], slot0_i[:, :, :]))
            V.tensor_scalar(slot_end[:, :, :], slot0[:, :, :], float(CAP), None, ALU.add
                            ).then_inc(dve_const, 1)

            def stats_of(gs):
                ts = slice(TG * gs[0], TG * (gs[-1] + 1))
                for g in gs:
                    dve.wait_ge(x_in_s[g], 16)
                    for t in range(TG * g, TG * g + TG):
                        last = V.bn_stats(stats[:, t, :], acc[:, t, :])
                then(last)
                for t in range(ts.start, ts.stop):
                    last = V.bn_aggr(mv[:, t, :], stats[:, t, :])
                then(last)
                V.tensor_scalar(ve[:, 0, ts], mv[:, ts, 1], LN_EPS, None, ALU.add)
                V.tensor_scalar(ve[:, 1, ts], mv[:, ts, 1], 1.0 + RMS_EPS, LN_EPS * RMS_EPS, ALU.mult, ALU.add
                                ).then_inc(ve_ready, 1)

            def rstd_of(gs):
                ts = slice(TG * gs[0], TG * (gs[-1] + 1))
                n = gs[0] // 2 + 1
                dve.wait_ge(root_ready, n)
                then(V.reciprocal(nw_a[:, :, ts], root[:, :, ts]))
                then(V.tensor_tensor(nw_b[:, :, ts], nw_a[:, :, ts], ve[:, :, ts], ALU.mult))
                then(V.scalar_tensor_tensor(out=nw_c[:, :, ts], in0=nw_b[:, :, ts], scalar=0.25,
                                            in1=root[:, :, ts], op0=ALU.mult, op1=ALU.add))
                V.reciprocal(rstd[:, :, ts], nw_c[:, :, ts]).then_inc(rstd_ready, 1)
                dve.wait_ge(rstd_ready, n)
                V.scalar_tensor_tensor(out=nmr[:, ts], in0=mv[:, ts, 0], scalar=-1.0, in1=rstd[:, 0, ts],
                                       op0=ALU.mult, op1=ALU.mult).then_inc(nmr_ready, 1)

            def normalize(g):
                for t in range(TG * g, TG * g + TG // 2):
                    last = V.tensor_scalar(xn[:, t, 0:D], acc[:, t, :], mv[:, t, 0:1], rstd[:, 0, t:t + 1],
                                           ALU.subtract, ALU.mult)
                last.then_inc(xn_ready, 1)

            def turned_lo(g):
                cols = slice(S * g, S * g + S)
                dve.wait_ge(xnT_hi_s, g + 1)
                V.tensor_tensor(xnT_lo[:, cols], turn_b[g % 2][:, :], xnT_hi[:, cols].bitcast(F32),
                                ALU.subtract).then_inc(xnT_ready, 1)

            stats_of((0, 1))
            rstd_of((0, 1))
            normalize(0)
            normalize(1)
            dve.wait_ge(rwT_hi_s, 1)
            V.tensor_tensor(rwT[:, E:2 * E], rw_ps, rwT[:, 0:E].bitcast(F32), ALU.subtract
                            ).then_inc(rwT_ready, 1)
            stats_of((2, 3))
            turned_lo(0)
            rstd_of((2, 3))
            normalize(2)
            normalize(3)
            turned_lo(1)
            dve.wait_ge(rstd_ready, B // 2)
            mark(V.tensor_tensor(std[:, :], ve[:, 0, :], rstd[:, 0, :], ALU.mult))
            turned_lo(2)
            settle()
            mark(V.tensor_tensor(rms[:, :], std[:, :], rstd[:, 1, :], ALU.mult))
            turned_lo(3)
            settle()

            def per_token(ap):
                return ap.rearrange("p (t o) -> p t o", o=1).to_broadcast([P, NT, E])

            ids = e_ids[:, :].rearrange("p (o e) -> p o e", o=1).to_broadcast([P, NT, E])

            def route_logits():
                dve.wait_ge(lg_copied, 1)
                then(V.tensor_tensor(z2[:, :, :], lg[:, :, 0:E], lg[:, :, E:2 * E], ALU.add))
                then(V.tensor_tensor(z[:, :, :], z2[:, :, :], per_token(rms[:, :]), ALU.mult))
                mark(V.tensor_reduce(m1[:, :], z[:, :, :], AX_X, ALU.max))

            def route_best():
                settle()
                then(V.tensor_tensor(z2[:, :, :], z[:, :, :], per_token(m1[:, :]), ALU.subtract))
                then(V.tensor_scalar(z[:, :, :], z2[:, :, :], -87.5, None, ALU.max))
                mark(V.tensor_scalar(z2[:, :, :], z[:, :, :], 0.0, float(E), ALU.is_lt, ALU.mult))

            def route_first():
                settle()
                then(V.tensor_tensor(key[:, :, :], z2[:, :, :], ids, ALU.add))
                then(V.tensor_reduce(i1[:, :], key[:, :, :], AX_X, ALU.min))
                mark(V.tensor_tensor(chosen[:, 0, :, :], ids, per_token(i1[:, :]), ALU.is_equal))

            def route_next():
                settle()
                then(V.scalar_tensor_tensor(out=z2[:, :, :], in0=chosen[:, 0, :, :], scalar=-1000.0, in1=z[:, :, :],
                                            op0=ALU.mult, op1=ALU.add))
                V.tensor_reduce(m2[:, :], z2[:, :, :], AX_X, ALU.max).then_inc(e2_asked, 1)
                dve.wait_ge(e2_asked, 1)
                mark(V.tensor_tensor(key[:, :, :], z2[:, :, :], per_token(m2[:, :]), ALU.is_lt))

            def route_second():
                settle()
                then(V.scalar_tensor_tensor(out=z2[:, :, :], in0=key[:, :, :], scalar=float(E), in1=ids,
                                            op0=ALU.mult, op1=ALU.add))
                mark(V.tensor_reduce(i2[:, :], z2[:, :, :], AX_X, ALU.min))

            def route_chosen():
                settle()
                then(V.tensor_tensor(chosen[:, 1, :, :], ids, per_token(i2[:, :]), ALU.is_equal))
                V.tensor_tensor(sel[:, :, :].rearrange("p e t -> p t e"), chosen[:, 0, :, :], chosen[:, 1, :, :], ALU.add
                                ).then_inc(sel_ready, 1)

            def route_slots():
                flat = lambda a: a.rearrange("p e t -> p (e t)")
                dve.wait_ge(rank_done, 1)
                then(V.tensor_tensor_scan(flat(incl[:, :, :]), seg[:, :], tot_ps, 0.0, ALU.mult, ALU.add))
                V.tensor_tensor(pos[:, :, :], incl[:, :, :], rank_ps, ALU.add).then_inc(pos_ready, 1)
                dve.wait_ge(pos_ready, 1)
                then(V.tensor_tensor(over[:, :, :], pos[:, :, :], slot_end[:, :, :], ALU.is_ge))
                then(V.scalar_tensor_tensor(out=flat(slot[:, :, :]), in0=flat(over[:, :, :]),
                                            scalar=float(2 * ZROW), in1=flat(pos[:, :, :]),
                                            op0=ALU.mult, op1=ALU.add))
                for k in range(2):
                    last = V.tensor_tensor(pick[:, k, :, :], chosen[:, k, :, :],
                                           slot[:, :, :].rearrange("p e t -> p t e"), ALU.mult)
                then(last)
                then(V.tensor_reduce(slot_f[:, :, :], pick[:, :, :, :], AX_X, ALU.add))
                V.tensor_scalar(slot_i[:, :, :], slot_f[:, :, :], float(ZROW), None, ALU.min
                                ).then_inc(slots_ready, 1)

            def route_weights():
                dve.wait_ge(e2_ready, 1)
                then(V.tensor_scalar(e2p[:, :], e2[:, :], 1.0, None, ALU.add))
                then(V.reciprocal(wgt[:, 0, :], e2p[:, :]))
                then(V.tensor_tensor(wgt[:, 1, :], wgt[:, 0, :], e2[:, :], ALU.mult))

            def y_lo(g):
                cols = slice(S * g, S * g + S)
                ps = turn_b[g % 2]
                dve.wait_ge(y_hi_s, g + 1)
                V.tensor_tensor(yR[R:2 * R, cols], ps[R:2 * R, :], yL[R:2 * R, cols].bitcast(F32),
                                ALU.subtract)
                V.tensor_tensor(yL[2 * R:3 * R, cols], ps[2 * R:3 * R, :],
                                yR[2 * R:3 * R, cols].bitcast(F32), ALU.subtract)

            def n_lo(g):
                cols = slice(S * g, S * g + S)
                dve.wait_ge(nhi_ready, g + 1)
                V.scalar_tensor_tensor(out=yR[3 * R:3 * R + 2, cols], in0=nhi[3 * R:3 * R + 2, :].bitcast(F32),
                                       scalar=row97[3 * R:3 * R + 2, 0:1],
                                       in1=turn_b[g % 2][3 * R:3 * R + 2, :],
                                       op0=ALU.mult, op1=ALU.add).then_inc(y_ready, 1)

            def add_attention(b, h):
                dve.wait_ge(att_done, 2 * b + h + 1)
                o = down_b[h][:, 0:2 * (D + 1)].rearrange("p (r c) -> p r c", r=2)
                t = TG * b + 2 * h
                then(V.reciprocal(rden[:, t:t + 2], o[:, :, D]))
                for r in range(2):
                    last = V.scalar_tensor_tensor(out=acc[:, t + r, :], in0=o[:, r, 0:D],
                                                  scalar=rden[:, t + r:t + r + 1], in1=acc[:, t + r, :],
                                                  op0=ALU.mult, op1=ALU.add)
                last.then_inc(att_added, 1)

            def mult_chunk(q, n, hid):
                dve.wait_ge(silu_ready, q + 1)
                V.tensor_tensor(hid, up_b[q % 2][:, 0:n], silu[:, q % 2, 0:n], ALU.mult).then_inc(hid_ready, 1)

            def slots_lo(e):
                dve.wait_ge(xg_hi_s, e + 1)
                V.tensor_tensor(xgT_lo[:, e % 2, :], turn_b[e % 2][:, 0:CAP],
                                xgT_hi[:, e % 2, :].bitcast(F32), ALU.subtract).then_inc(xg_ready, 1)

            def block_sum(b):
                dve.wait_ge(job_done, block_job(b) + 1)
                if b == B - 1:
                    dve.wait_ge(summed, NT)
                elif b > 0:
                    dve.wait_ge(att_added, 2 * (b + 1))
                a = acc[:, TG * b:TG * b + TG, :].rearrange("p t d -> p (t d)")
                V.tensor_tensor(a, down_b[block_job(b) % 2][:, :], a, ALU.add).then_inc(block_added, 1)

            def mult_of_block(b, c):
                if b >= 2 and c == 0:
                    dve.wait_ge(job_done, block_job(b - 2) + 1)
                mult_chunk(block_chunk(b) + c, S, hid_s[:, b % 2, c, :])

            def add_gathered(t):
                if t < 3 * TG:
                    dve.wait_ge(block_added, t // TG + 1)
                dve.wait_ge(gathered[t], 32)
                then(V.scalar_tensor_tensor(out=acc[:, t, :], in0=got[:, t, 0, :], scalar=wgt[:, 0, t:t + 1],
                                            in1=acc[:, t, :], op0=ALU.mult, op1=ALU.add))
                V.scalar_tensor_tensor(out=acc[:, t, :], in0=got[:, t, 1, :], scalar=wgt[:, 1, t:t + 1],
                                       in1=acc[:, t, :], op0=ALU.mult, op1=ALU.add).then_inc(summed, 1)

            route_logits()
            mult_of_block(0, 0)
            route_best()
            mult_of_block(0, 1)
            route_first()
            mult_of_block(0, 2)
            route_next()
            mult_of_block(0, 3)
            route_second()
            route_chosen()
            mult_of_block(0, 4)
            y_lo(0)
            mult_of_block(0, 5)
            n_lo(0)
            mult_of_block(0, 6)
            mult_of_block(0, 7)
            route_slots()
            route_weights()
            y_lo(1)
            n_lo(1)
            y_lo(2)
            block_sum(0)
            dve.wait_ge(block_added, 1)
            n_lo(2)
            y_lo(3)
            add_attention(0, 0)
            n_lo(3)
            add_attention(0, 1)
            for b in range(1, B):
                add_attention(b, 0)
                add_attention(b, 1)
            for c in range(CS):
                mult_of_block(1, c)
            slots_lo(0)
            for e in range(E):
                if e + 1 < E:
                    slots_lo(e + 1)
                if e >= 2:
                    dve.wait_ge(job_done, expert_job(e - 2) + 1)
                for c in range(CR):
                    mult_chunk(expert_chunk(e) + c, CAP, hid_e[:, e % 2, c, :])
            for c in range(CS):
                mult_of_block(2, c)
                if c == 0:
                    block_sum(1)
            for c in range(CS):
                mult_of_block(3, c)
                add_gathered(c)
            block_sum(2)
            for t in range(CS, 3 * TG):
                add_gathered(t)
            for t in range(3 * TG, NT):
                add_gathered(t)
            block_sum(3)

        @block.tensor
        def _(pe):
            M = nc.tensor.matmul

            def parts(o, w_hi, w_lo, m_hi, m_lo):
                M(o, w_hi, m_hi, start=True, stop=False)
                M(o, w_hi, m_lo, start=False, stop=False)
                return M(o, w_lo, m_hi, start=False, stop=True)

            def turn(g):
                pe.wait_ge(xn_ready, g + 1)
                pe.wait_ge(xn_ready_act, g + 1)
                if g >= 2:
                    pe.wait_ge(xnT_ready, g - 1)
                for j in range(TG):
                    last = nc.tensor.transpose(turn_b[g % 2][:, P * j:P * j + P], xn[:, TG * g + j, 0:D],
                                               ident[:, :])
                last.then_inc(xnT_turned, 1)

            def logits(g):
                pe.wait_ge(xnT_ready, g + 1)
                for t in range(TG * g, TG * g + TG):
                    M(lg_ps[:, t, :], xnT_hi[:, P * t:P * t + P], rwT[:, :], start=True, stop=False)
                    last = M(lg_ps[:, t, :], xnT_lo[:, P * t:P * t + P], rwT[:, :], start=False, stop=True)
                last.then_inc(lg_done, 1)

            def project(g):
                cols = slice(S * g, S * g + S)
                if g < 2:
                    pe.wait_ge(xnT_ready, B + g - 1)
                else:
                    pe.wait_ge(y_ready, g - 1)
                parts(turn_b[g % 2][0:3 * R, :], U_hi[:, :, :].rearrange("p j r -> p (j r)"),
                      U_lo[:, :, :].rearrange("p j r -> p (j r)"), xnT_hi[:, cols], xnT_lo[:, cols]
                      ).then_inc(y_done, 1)

            def norms(g):
                pe.wait_ge(ysq_ready, g + 1)
                M(turn_b[g % 2][3 * R:3 * R + 2, :], half[:, :], ysq[:, S * g:S * g + S], start=True, stop=True
                  ).then_inc(n_done, 1)

            def score(b, j):
                if b == 0:
                    pe.wait_ge(hid_ready, CS - 1 + j // 2)
                else:
                    pe.wait_ge(prob_ready, TG * (b - 1) + j + 1)
                if j == TG - 1:
                    pe.wait_ge(nb_copied, b + 1)
                M(bank[j][:, :], yL[0:3 * R + 2, S * b + P * j:S * b + P * j + P],
                  yR[0:3 * R + 2, S * b:S * b + S], start=True, stop=True).then_inc(score_done, 1)

            def first_scores(b):
                pe.wait_ge(y_ready, b + 1)
                for j in range(TG - 1):
                    score(b, j)
                if b == 0:
                    pe.wait_ge(hid_ready, CS)
                else:
                    pe.wait_ge(prob_ready, TG * b)
                for j in range(TG):
                    t = TG * b + j
                    last = M(nb_ps[:, j, :], ysq[:, P * t:P * t + P], half[:, :], start=True, stop=True)
                last.then_inc(nb_done, 1)

            def attend(b, h):
                pe.wait_ge(prob_ready, TG * (b + 1))
                if b >= 1:
                    pe.wait_ge(att_added, 2 * (b - 1) + h + 1)
                elif h == 0:
                    pe.wait_ge(block_added, 1)
                else:
                    pe.wait_ge(pos_ready, 1)
                for i in range(2 * h, 2 * h + 2):
                    for j in range(TG):
                        last = M(down_b[h][:, (D + 1) * (i % 2):(D + 1) * (i % 2 + 1)],
                                 probs[:, b % 2, j, P * i:P * i + P], xn[:, TG * b + j, :],
                                 start=(j == 0), stop=(j == TG - 1))
                last.then_inc(att_done, 1)

            def ranks():
                pe.wait_ge(sel_ready, 1)
                s = sel[:, :, :].rearrange("p e t -> p (e t)")
                M(bank[5][:, rank_cols], tri[:, :], s, start=True, stop=False)
                M(bank[5][:, rank_cols], ones_f[0:1, :], slot0[0:1, :, :].rearrange("p e t -> p (e t)"),
                  start=False, stop=True)
                M(tot_ps, ones_bf[:, :], s, start=True, stop=True).then_inc(rank_done, 1)

            def up_chunk(q, n, w_hi, w_lo, m_hi, m_lo):
                if q >= 2:
                    pe.wait_ge(silu_ready, q - 1)
                parts(gate_b[q % 2][:, 0:n], w_hi(0), w_lo(0), m_hi, m_lo)
                if q >= 2:
                    pe.wait_ge(hid_ready, q - 1)
                parts(up_b[q % 2][:, 0:n], w_hi(1), w_lo(1), m_hi, m_lo).then_inc(chunk_done, 1)

            def up_block(b, cs=range(CS)):
                for c in cs:
                    if b == 0:
                        pe.wait_ge(sw_ready, c // 2 + 1)
                    up_chunk(block_chunk(b) + c, S, lambda w: sw_hi[:, w, P * c:P * c + P],
                             lambda w: sw_lo[:, w, P * c:P * c + P],
                             xnT_hi[:, S * b:S * b + S], xnT_lo[:, S * b:S * b + S])

            def bank_free(job):
                if job == 0:
                    pe.wait_ge(rwT_ready, 1)
                elif job <= 2:
                    pe.wait_ge(att_added, 2 * B)
                elif job - 2 <= E:
                    pe.wait_ge(eo_ready, job - 2)
                else:
                    pe.wait_ge(block_added, job - 2 - E + 1)

            def down_block(b):
                job = block_job(b)
                bank_free(job)
                if b == 0:
                    pe.wait_ge(sd_loaded, 16)
                pe.wait_ge(hid_ready, block_chunk(b) + CS)
                for i in range(TG):
                    for c in range(CS):
                        last = M(down_b[job % 2][:, D * i:D * i + D], hid_s[:, b % 2, c, P * i:P * i + P],
                                 sd[:, c, :], start=(c == 0), stop=(c == CS - 1))
                last.then_inc(job_done, 1)

            def turn_slots(e):
                s = e % 2
                pe.wait_ge(xg_loaded[s], 32 * (e // 2 + 1))
                if e >= 2:
                    pe.wait_ge(xg_ready, e - 1)
                for r in range(3):
                    n = P if r < 2 else TAIL
                    last = nc.tensor.transpose(turn_b[s][:, P * r:P * r + n], xg[0:n, s, r, :],
                                               ident[0:n, 0:n])
                last.then_inc(xg_turned, 1)

            def up_expert(e):
                s = e % 2
                pe.wait_ge(ew_ready, e + 1)
                pe.wait_ge(xg_ready, e + 1)
                for c in range(CR):
                    up_chunk(expert_chunk(e) + c, CAP, lambda w: ew_hi[:, s, w, P * c:P * c + P],
                             lambda w: ew_lo[:, s, w, P * c:P * c + P], xgT_hi[:, s, :], xgT_lo[:, s, :])

            def down_expert(e):
                job = expert_job(e)
                bank_free(job)
                pe.wait_ge(rd_loaded[e % 3], 16 * (e // 3 + 1))
                pe.wait_ge(hid_ready, expert_chunk(e) + CR)
                for r in range(3):
                    n = P if r < 2 else TAIL
                    for c in range(CR):
                        last = M(down_b[job % 2][0:n, D * r:D * r + D], hid_e[:, e % 2, c, P * r:P * r + n],
                                 rd[:, e % 3, c, :], start=(c == 0), stop=(c == CR - 1))
                last.then_inc(job_done, 1)

            pe.wait_ge(consts, 1)
            pe.wait_ge(rw_loaded, 16)
            nc.tensor.transpose(rw_ps, rw_raw[:, :], ident[0:E, 0:E]).then_inc(rwT_turned, 1)
            turn(0)
            turn(1)
            pe.wait_ge(rwT_ready, 1)
            logits(0)
            logits(1)
            turn(2)
            turn(3)
            logits(2)
            logits(3)
            up_block(0, range(0, 2))
            pe.wait_ge(U_ready, 1)
            pe.wait_ge(dve_const, 1)
            project(0)
            up_block(0, range(2, 4))
            project(1)
            norms(0)
            up_block(0, range(4, 6))
            norms(1)
            up_block(0, range(6, CS))
            ranks()
            first_scores(0)
            project(2)
            score(0, TG - 1)
            down_block(0)
            norms(2)
            project(3)
            for b in range(B):
                if b + 1 < B:
                    first_scores(b + 1)
                attend(b, 0)
                if b + 1 < B:
                    score(b + 1, TG - 1)
                if b == 0:
                    norms(3)
                attend(b, 1)
            up_block(1)
            turn_slots(0)
            for e in range(E):
                if e + 1 < E:
                    turn_slots(e + 1)
                up_expert(e)
                if e >= 1:
                    down_expert(e - 1)
            down_expert(E - 1)
            down_block(1)
            up_block(2)
            up_block(3)
            down_block(2)
            down_block(3)


_INS = ['L0_attn_x', 'L0_attn_U', 'L0_ffn_router_w', 'L0_ffn_rg', 'L0_ffn_ru', 'L0_ffn_rd',
        'L0_ffn_sg', 'L0_ffn_su', 'L0_ffn_sd']
_OUTS = [((4, 512, 128), 'float32')]


def kernel(**inputs):
    import numpy as _np
    import concourse.bacc as _bacc
    from concourse import mybir as _mybir
    from concourse.bass_utils import run_bass_kernel_spmd as _run

    nc = _bacc.Bacc("TRN2", target_bir_lowering=False, num_devices=1)
    arrays, args = {}, []
    for name in _INS:
        a = _np.ascontiguousarray(inputs[name])
        arrays[f"in_{name}_dram"] = a
        args.append(nc.dram_tensor(f"in_{name}_dram", a.shape, _mybir.dt.from_np(a.dtype), kind="ExternalInput").ap())
    for i, (shape, dtype) in enumerate(_OUTS):
        dt = _mybir.dt.from_np(_np.dtype(dtype))
        args.append(nc.dram_tensor(f"out_{i}_dram", shape, dt, kind="ExternalOutput").ap())
    moe_attention_kernel(nc, *args)
    r = _run(nc, [arrays], core_ids=[0])
    got = tuple(r.results[0][f"out_{i}_dram"] for i in range(len(_OUTS)))
    return got[0]
```

```python
from contextlib import ExitStack

import concourse.bass as bass
from concourse import mybir

ALU = mybir.AluOpType
ACT = mybir.ActivationFunctionType
AX_X = mybir.AxisListType.X
F32 = mybir.dt.float32
F32R = mybir.dt.float32r
BF16 = mybir.dt.bfloat16
I32 = mybir.dt.int32

P = 128
LN_EPS = 1e-5
RMS_EPS = 1.1920928955078125e-07
CAP_FACTOR = 1.25
TOP_K = 2


def moe_attention_kernel(nc, x_in, U_in, rw_in, rg_in, ru_in, rd_in, sg_in, su_in, sd_in, out):
    B, S, D = x_in.shape
    R = U_in.shape[1]
    E, _, IR = rg_in.shape
    IS = sg_in.shape[1]
    assert D == P and S == 512 and R == 32 and TOP_K == 2
    T = B * S
    NT = T // P
    TG = S // P
    CAP = max(int(CAP_FACTOR * T / E), 1)
    CR = IR // P
    CS = IS // P
    NO_SLOT = E * CAP
    TAIL = CAP - 2 * P
    assert 0 < TAIL <= P and E <= 8
    PASSES = [(0,), (1,), (2, 3)]
    pass_of = [i for i, gs in enumerate(PASSES) for _ in gs]
    assert len(pass_of) == B
    WARMING = 60
    EARLY = B - 1
    RW = D + 2
    XB = 5

    PARTS = 2
    WIDE = range(1, EARLY)
    NR = slice(3 * R, 3 * R + 4)

    def block_job(b):
        return b if b < EARLY else b + E

    def block_chunk(b):
        return CS * b if b < EARLY else CS * b + CR * E

    def expert_job(e):
        return EARLY + e

    def expert_chunk(e):
        return CS * EARLY + CR * e

    def wide_chunk(b, c):
        return CS * (b - WIDE[0]) + c

    def wide_of(q):
        w = q - block_chunk(WIDE[0])
        return w if 0 <= w < CS * len(WIDE) else None

    slots_dram = nc.dram_tensor("slots_dram", (E * CAP, RW), F32).ap()
    routed_dram = nc.dram_tensor("routed_dram", (2 * T, D), F32).ap()

    x_v = x_in.rearrange("b (t p) d -> b p t d", p=P)
    out_v = out.rearrange("b (t p) d -> b p t d", p=P)
    routed_v = routed_dram.rearrange("(k b t p) d -> k b p t d", k=2, b=B, p=P)

    with ExitStack() as ctx:
        def sb(name, shape, dt=F32):
            return ctx.enter_context(nc.sbuf_tensor(name, shape, dt))

        def sem(name):
            return ctx.enter_context(nc.semaphore(name))

        acc = sb("acc", [P, NT, D])
        row1 = sb("row1", [P, NT, RW + 1])
        row2 = sb("row2", [P, NT, RW])
        xn = row1[:, :, 2:RW]
        xn_ones = row1[:, :, 2:RW + 1]
        xnT_hi = sb("xnT_hi", [P, T], F32R)
        xnT_lo = sb("xnT_lo", [P, T], F32R)
        ident = sb("ident", [P, P])
        fill = sb("fill", [P, RW])
        minus_ones = sb("minus_ones", [P, P])
        tri = sb("tri", [P, P], BF16)
        ones_bf = sb("ones_bf", [P, P], BF16)
        ones_f = sb("ones_f", [P, P])
        e_ids = sb("e_ids", [P, E])
        e_ids_i = sb("e_ids_i", [P, E], I32)
        from_lo = sb("from_lo", [P, 1])
        minus_lo = sb("minus_lo", [P, 1])
        first_two = sb("first_two", [P, 1])
        last_two = sb("last_two", [P, 1])
        seg = sb("seg", [P, E * NT])
        slot0_i = sb("slot0_i", [P, E, NT], I32)
        slot0 = sb("slot0", [P, E, NT])
        slot_end = sb("slot_end", [P, E, NT])
        half = sb("half", [R, 4])
        rw_raw = sb("rw_raw", [E, D])
        rwT = sb("rwT", [P, 2 * B - 1, P // B], F32R)
        lgT = sb("lgT", [P, S])
        fold = sb("fold", [P, B, E])
        U_raw = sb("U_raw", [P, R])
        U_hi = sb("U_hi", [P, 3, R], F32R)
        U_lo = sb("U_lo", [P, 3, R], F32R)
        yL = sb("yL", [P, T], F32R)
        yR = sb("yR", [P, T], F32R)
        ysq = sb("ysq", [R, T])
        norm_parts = sb("norm_parts", [P, S], F32R)
        rden = sb("rden", [P, NT])
        stats = sb("stats", [P, NT, 6])
        mv = sb("mv", [P, NT, 2])
        ve = sb("ve", [P, 2, NT])
        root = sb("root", [P, 2, NT])
        nw_a = sb("nw_a", [P, 2, NT])
        nw_b = sb("nw_b", [P, 2, NT])
        nw_c = sb("nw_c", [P, 2, NT])
        rstd = sb("rstd", [P, 2, NT])
        nmr = sb("nmr", [P, NT])
        std = sb("std", [P, NT])
        rms = sb("rms", [P, NT])
        z = sb("z", [P, NT, E])
        z2 = sb("z2", [P, NT, E])
        key = sb("key", [P, NT, E])
        chosen = sb("chosen", [P, 2, NT, E])
        sel = sb("sel", [P, E, NT], BF16)
        m1 = sb("m1", [P, NT])
        m2 = sb("m2", [P, NT])
        i1 = sb("i1", [P, NT])
        i2 = sb("i2", [P, NT])
        e2 = sb("e2", [P, NT])
        e2p = sb("e2p", [P, NT])
        incl = sb("incl", [P, E, NT])
        pos = sb("pos", [P, E, NT])
        over = sb("over", [P, E, NT])
        slot = sb("slot", [P, E, NT])
        pick = sb("pick", [P, 2, NT, E])
        slot_f = sb("slot_f", [P, 2, NT])
        slot_i = sb("slot_i", [P, 2, NT], I32)
        sw_raw = sb("sw_raw", [P, 2, IS])
        sw_hi = sb("sw_hi", [P, 2, IS], F32R)
        sw_lo = sb("sw_lo", [P, 2, IS], F32R)
        sd = sb("sd", [P, CS, D])
        ew_raw = sb("ew_raw", [P, 2, 2, IR])
        ew_hi = sb("ew_hi", [P, 2, 2, IR], F32R)
        ew_lo = sb("ew_lo", [P, 2, 2, IR], F32R)
        rd = sb("rd", [P, 3, CR, D])
        xg = sb("xg", [P, XB, 3, RW])
        xgT_hi = sb("xgT_hi", [P, 2, CAP], F32R)
        xgT_lo = sb("xgT_lo", [P, 2, CAP], F32R)
        silu = sb("silu", [P, 2, S])
        hid_s = sb("hid_s", [P, 2, CS, S])
        hid_e = sb("hid_e", [P, 2, CR, CAP])
        assert CS == 2 * TG and B % 2 == 0
        probs = hid_s[:, 1, :, :].rearrange("p (b j) i -> p b j i", b=2)
        assert PARTS * S + CS * D <= T
        hid_hi, hid_lo = [t[:, 0:PARTS * S].rearrange("p (w i) -> p w i", w=PARTS) for t in (yL, yR)]
        sd_hi, sd_lo = [t[:, PARTS * S:PARTS * S + CS * D].rearrange("p (c d) -> p c d", c=CS)
                        for t in (yL, yR)]
        turned_out = sb("turned_out", [P, S])
        eo = sb("eo", [P, 2, 3, D])
        routed = [row1[:, :, 2:RW], row2[:, :, 2:RW]]

        bank = [ctx.enter_context(nc.psum_tensor(f"bank{i}", [P, 512], F32)) for i in range(8)]
        gate_b = [bank[0], bank[2]]
        up_b = [bank[1], bank[3]]
        down_b = [bank[4], bank[5]]
        turn_b = [bank[6], bank[7]]
        rw_ps = bank[4][:, 64:64 + E]
        assert 4 * E == P // B
        lg_ps = bank[5][:, 0:NT * E]
        rank_cols = slice(NT * 2 * E, NT * 3 * E)
        rank_ps = bank[5][:, rank_cols].rearrange("p (e t) -> p e t", e=E)
        tot_ps = bank[5][:, NT * 3 * E:NT * 4 * E]

        x_in_s = [sem(f"x_loaded{g}") for g in range(B)]
        rw_loaded, U_loaded = sem("rw_loaded"), sem("U_loaded")
        sw_loaded = [sem(f"sw_loaded{h}") for h in range(2)]
        sd_loaded = sem("sd_loaded")
        ew_loaded = [sem(f"ew_loaded{i}") for i in range(2)]
        rd_loaded = [sem(f"rd_loaded{i}") for i in range(3)]
        xg_loaded = [sem(f"xg_loaded{i}") for i in range(2)]
        slots_emptied = sem("slots_emptied")
        scattered = sem("scattered")
        eo_written = [sem(f"eo_written{i}") for i in range(2)]
        routed_loaded = [sem(f"routed_loaded{g}") for g in range(B)]
        row2_copied = sem("row2_copied")
        routed_zeroed = sem("routed_zeroed")
        out_written = sem("out_written")
        pool_step = sem("pool_step")
        consts = sem("consts")
        fill_set, fill_zeroed = sem("fill_set"), sem("fill_zeroed")
        ones_set = sem("ones_set")
        wgt_ready = sem("wgt_ready")
        dve_const = sem("dve_const")
        dve_step = sem("dve_step")
        ve_ready = sem("ve_ready")
        root_ready = sem("root_ready")
        rstd_ready, nmr_ready = sem("rstd_ready"), sem("nmr_ready")
        xn_ready = sem("xn_ready")
        xn_ready_act = sem("xn_ready_act")
        rwT_zeroed = sem("rwT_zeroed")
        rwT_turned, rwT_hi_s, rwT_ready = sem("rwT_turned"), sem("rwT_hi_s"), sem("rwT_ready")
        U_hi_s, U_ready = sem("U_hi_s"), sem("U_ready")
        xnT_turned, xnT_hi_s, xnT_ready = sem("xnT_turned"), sem("xnT_hi_s"), sem("xnT_ready")
        lgT_done, lgT_copied, lg_done = sem("lgT_done"), sem("lgT_copied"), sem("lg_done")
        y_done, y_hi_s, y_ready = sem("y_done"), sem("y_hi_s"), sem("y_ready")
        ysq_ready, n_done, nhi_ready = sem("ysq_ready"), sem("n_done"), sem("nhi_ready")
        norm_split, yL_ready = sem("norm_split"), sem("yL_ready")
        e2_asked, e2_ready = sem("e2_asked"), sem("e2_ready")
        sel_ready, rank_done = sem("sel_ready"), sem("rank_done")
        pos_ready = sem("pos_ready")
        slots_ready = sem("slots_ready")
        score_done, prob_ready = sem("score_done"), sem("prob_ready")
        att_done, att_added = sem("att_done"), sem("att_added")
        sw_hi_s, sw_ready = sem("sw_hi_s"), sem("sw_ready")
        ew_hi_s, ew_ready = sem("ew_hi_s"), sem("ew_ready")
        xg_turned, xg_hi_s, xg_ready = sem("xg_turned"), sem("xg_hi_s"), sem("xg_ready")
        chunk_done, silu_ready, hid_ready = sem("chunk_done"), sem("silu_ready"), sem("hid_ready")
        job_done = sem("job_done")
        sd_hi_s, sd_split = sem("sd_hi_s"), sem("sd_split")
        hid_hi_s, hid_split, parts_used = sem("hid_hi_s"), sem("hid_split"), sem("parts_used")
        out_copied = sem("out_copied")
        block_added, eo_ready = sem("block_added"), sem("eo_ready")
        summed = sem("summed")

        block = ctx.enter_context(nc.Block())

        @block.sync
        def _(sp):
            def load_expert_weights(e, s):
                sp.dma_start(ew_raw[:, s, 0, :], rg_in[e]).then_inc(ew_loaded[s], 16)
                sp.dma_start(ew_raw[:, s, 1, :], ru_in[e]).then_inc(ew_loaded[s], 16)

            def load_down(e, s):
                sp.dma_start(rd[:, s, :, :], rd_in[e].rearrange("(c p) d -> p c d", p=P)
                             ).then_inc(rd_loaded[s], 16)

            def load_slots(e, s):
                rows = slots_dram[e * CAP:(e + 1) * CAP, :]
                sp.dma_start(xg[:, e % XB, 0:2, :], rows[0:2 * P, :].rearrange("(p r) d -> p r d", r=2)
                             ).then_inc(xg_loaded[s], 16)
                sp.dma_start(xg[0:TAIL, e % XB, 2, :], rows[2 * P:CAP, :]).then_inc(xg_loaded[s], 16)

            def load_x(g):
                sp.dma_start(acc[:, TG * g:TG * g + TG, :], x_v[g]).then_inc(x_in_s[g], 16)

            def load_shared(h):
                cols = slice(IS // 2 * h, IS // 2 * (h + 1))
                sp.dma_start(sw_raw[:, 0, cols], sg_in[:, cols]).then_inc(sw_loaded[h], 16)
                sp.dma_start(sw_raw[:, 1, cols], su_in[:, cols]).then_inc(sw_loaded[h], 16)

            load_x(0)
            load_x(1)
            load_shared(0)
            for g in range(2, B):
                load_x(g)
            sp.dma_start(rw_raw[:, :], rw_in).then_inc(rw_loaded, 16)
            sp.dma_start(U_raw[:, :], U_in).then_inc(U_loaded, 16)
            load_shared(1)
            sp.wait_ge(fill_set, 1)
            sp.wait_ge(fill_zeroed, 1)
            sp.dma_start(slots_dram.rearrange("(p a) d -> p a d", p=P),
                         fill[:, :].rearrange("p (o d) -> p o d", o=1).to_broadcast([P, E * CAP // P, RW])
                         ).then_inc(slots_emptied, 16)
            sp.dma_start(sd[:, :, :], sd_in.rearrange("(c p) d -> p c d", p=P)).then_inc(sd_loaded, 16)
            sp.wait_ge(xn_ready, B)
            sp.wait_ge(xn_ready_act, B)
            sp.dma_start(row2[:, :, 2:RW], xn).then_inc(row2_copied, 16)
            for e in range(2):
                load_expert_weights(e, e)
                load_down(e, e)
            sp.dma_start(routed_dram.rearrange("(p a) d -> p a d", p=P),
                         fill[:, 2:RW].rearrange("p (o d) -> p o d", o=1).to_broadcast([P, 2 * T // P, D])
                         ).then_inc(routed_zeroed, 16)
            sp.wait_ge(scattered, 16 * 2 * NT)
            for e in range(2):
                load_slots(e, e)
            for e in range(E - 2):
                sp.wait_ge(ew_ready, e + 1)
                load_expert_weights(e + 2, e % 2)
                sp.wait_ge(xg_turned, e + 1)
                if e + 2 >= XB:
                    before = e + 2 - XB
                    sp.wait_ge(eo_written[before % 2], 48 * (before // 2 + 1))
                load_slots(e + 2, e % 2)
                if e >= 1:
                    sp.wait_ge(job_done, expert_job(e - 1) + 1)
                load_down(e + 2, (e + 2) % 3)
            for i in range(2):
                sp.wait_ge(eo_written[i], 48 * ((E - i + 1) // 2))
            for g in range(B):
                for k in range(2):
                    sp.dma_start(routed[k][:, TG * g:TG * g + TG, :], routed_v[k, g]
                                 ).then_inc(routed_loaded[g], 16)
            for g in range(B - 1):
                sp.wait_ge(summed, g + 1)
                sp.dma_start(out_v[g], acc[:, TG * g:TG * g + TG, :]).then_inc(out_written, 16)
            for h in range(2):
                sp.wait_ge(block_added, B + h)
                sp.dma_start(out_v[B - 1][:, 2 * h:2 * h + 2, :],
                             acc[:, TG * (B - 1) + 2 * h:TG * (B - 1) + 2 * h + 2, :]).then_inc(out_written, 16)
            sp.wait_ge(out_written, 16 * (B + 1))

        @block.gpsimd
        def _(pool):
            steps = [0]

            def after(ins):
                steps[0] += 1
                ins.then_inc(pool_step, 1)
                pool.wait_ge(pool_step, steps[0])

            G = nc.gpsimd
            G.iota(fill[:, 1:2].bitcast(I32), pattern=[[0, 1]], base=2 * T, channel_multiplier=0
                   ).then_inc(fill_set, 1)
            G.memset(minus_ones[:, :], -1.0)
            after(G.memset(ones_f[:, :], 1.0))
            G.affine_select(out=ident[:, :], in_=ones_f[:, :], compare_op=ALU.is_equal,
                            fill=0.0, base=0, pattern=[[-1, P]], channel_multiplier=1)
            G.affine_select(out=tri[:, :], in_=minus_ones[:, :], compare_op=ALU.is_ge,
                            fill=0.0, base=0, pattern=[[-1, P]], channel_multiplier=1)
            G.iota(slot0_i[:, :, :], pattern=[[CAP, E], [0, NT]], base=0, channel_multiplier=0)
            G.iota(e_ids_i[:, :], pattern=[[1, E]], base=0, channel_multiplier=0)
            K0 = 3 * R
            G.affine_select(out=first_two[:, :], in_=ones_f[:, 0:1], compare_op=ALU.is_ge,
                            fill=0.0, base=K0 + 1, pattern=[[0, 1]], channel_multiplier=-1)
            G.affine_select(out=last_two[:, :], in_=ones_f[:, 0:1], compare_op=ALU.is_ge,
                            fill=0.0, base=-(K0 + 2), pattern=[[0, 1]], channel_multiplier=1)
            after(G.affine_select(out=from_lo[:, :], in_=minus_ones[:, 0:1], compare_op=ALU.is_ge,
                                  fill=0.0, base=-(K0 + 1), pattern=[[0, 1]], channel_multiplier=1))
            G.affine_select(out=minus_lo[:, :], in_=from_lo[:, :], compare_op=ALU.is_ge,
                            fill=0.0, base=K0 + 2, pattern=[[0, 1]], channel_multiplier=-1)
            G.affine_select(out=seg[:, :].rearrange("p (e t) -> p e t", e=E),
                            in_=ones_f[:, 0:E * NT].rearrange("p (e t) -> p e t", e=E),
                            compare_op=ALU.is_gt, fill=0.0, base=0,
                            pattern=[[0, E], [1, NT]], channel_multiplier=0).then_inc(consts, 1)
            G.iota(row1[:, :, 1].bitcast(I32), pattern=[[P, NT]], base=0, channel_multiplier=1)
            G.iota(row2[:, :, 1].bitcast(I32), pattern=[[P, NT]], base=T, channel_multiplier=1)
            for i in range(CS // 2):
                cols = slice(2 * P * i, 2 * P * (i + 1))
                pool.wait_ge(sw_hi_s, i + 1)
                G.tensor_tensor(sw_lo[:, :, cols], sw_raw[:, :, cols], sw_hi[:, :, cols].bitcast(F32),
                                ALU.subtract).then_inc(sw_ready, 1)
                if i == 1:
                    pool.wait_ge(U_hi_s, 1)
                    for j in range(3):
                        last = G.tensor_tensor(U_lo[:, j, :], U_raw[:, :], U_hi[:, j, :].bitcast(F32), ALU.subtract)
                    last.then_inc(U_ready, 1)
            pool.wait_ge(slots_emptied, 16)
            pool.wait_ge(xn_ready, B)
            pool.wait_ge(xn_ready_act, B)
            pool.wait_ge(row2_copied, 16)
            pool.wait_ge(wgt_ready, 1)
            pool.wait_ge(slots_ready, 1)
            for t in range(NT):
                for k, row in enumerate((row1, row2)):
                    G.indirect_dma_start(
                        slots_dram, bass.IndirectOffsetOnAxis(slot_i[:, k, t:t + 1], 0), row[:, t, 0:RW], None,
                        bounds_check=E * CAP - 1, oob_is_err=False).then_inc(scattered, 16)

            def split_weights(e):
                pool.wait_ge(ew_hi_s, 2 * (e + 1))
                G.tensor_tensor(ew_lo[:, e % 2, :, :], ew_raw[:, e % 2, :, :],
                                ew_hi[:, e % 2, :, :].bitcast(F32), ALU.subtract).then_inc(ew_ready, 1)

            def write_routed(e):
                pool.wait_ge(eo_ready, e + 1)
                for r in range(3):
                    n = P if r < 2 else TAIL
                    G.indirect_dma_start(
                        routed_dram, bass.IndirectOffsetOnAxis(xg[0:n, e % XB, r, 1:2].bitcast(I32), 0),
                        eo[0:n, e % 2, r, :], None,
                        bounds_check=2 * T - 1, oob_is_err=False).then_inc(eo_written[e % 2], 16)

            split_weights(0)
            split_weights(1)
            pool.wait_ge(routed_zeroed, 16)
            for e in range(1, E):
                if e + 1 < E:
                    split_weights(e + 1)
                write_routed(e - 1)
            write_routed(E - 1)

        @block.scalar
        def _(act):
            C = nc.scalar

            def root_of(gs):
                ts = slice(TG * gs[0], TG * (gs[-1] + 1))
                act.wait_ge(ve_ready, pass_of[gs[0]] + 1)
                C.activation(root[:, :, ts], ve[:, :, ts], ACT.Sqrt, scale=0.25).then_inc(root_ready, 1)

            def normalize(g):
                act.wait_ge(nmr_ready, pass_of[g] + 1)
                for t in range(TG * g + TG // 2, TG * g + TG):
                    last = C.activation(xn[:, t, :], acc[:, t, :], ACT.Identity, bias=nmr[:, t:t + 1],
                                        scale=rstd[:, 0, t:t + 1])
                last.then_inc(xn_ready_act, 1)

            def turned_hi(g):
                act.wait_ge(xnT_turned, g + 1)
                C.copy(xnT_hi[:, S * g:S * g + S], turn_b[g % 2][:, :]).then_inc(xnT_hi_s, 1)

            def y_hi(g):
                cols = slice(S * g, S * g + S)
                act.wait_ge(y_done, g + 1)
                C.copy(yL[0:3 * R, cols], turn_b[g % 2][0:3 * R, :])
                C.copy(yR[0:3 * R, cols], turn_b[g % 2][0:3 * R, :]).then_inc(y_hi_s, 1)
                C.activation(ysq[:, cols], turn_b[g % 2][0:R, :], ACT.Square).then_inc(ysq_ready, 1)

            def n_hi(g):
                act.wait_ge(n_done, g + 1)
                if g > 0:
                    act.wait_ge(y_ready, g)
                    act.wait_ge(yL_ready, g)
                C.copy(norm_parts[NR, :], turn_b[g % 2][NR, :]).then_inc(nhi_ready, 1)

            def n_left(g):
                act.wait_ge(norm_split, g + 1)
                C.activation(yL[NR, S * g:S * g + S], norm_parts[NR, :].bitcast(F32), ACT.Identity,
                             bias=first_two[NR, 0:1], scale=last_two[NR, 0:1]).then_inc(yL_ready, 1)

            def exps(b):
                for j in range(TG):
                    t = TG * b + j
                    act.wait_ge(score_done, t + 1)
                    if j == 0 and b >= 2:
                        act.wait_ge(att_done, 2 * (b - 1))
                    C.activation(probs[:, b % 2, j, :], bank[j][:, :], ACT.Exp, scale=2.0
                                 ).then_inc(prob_ready, 1)

            def silu_chunk(q, n):
                act.wait_ge(chunk_done, q + 1)
                if q >= 2 and wide_of(q - 2) is not None:
                    act.wait_ge(hid_split, wide_of(q - 2) + 1)
                elif q >= 2:
                    act.wait_ge(hid_ready, q - 1)
                C.activation(silu[:, q % 2, 0:n], gate_b[q % 2][:, 0:n], ACT.Silu).then_inc(silu_ready, 1)

            def split_hi(w):
                q = block_chunk(WIDE[0]) + w
                act.wait_ge(hid_ready, q + 1)
                if w >= PARTS:
                    act.wait_ge(parts_used, w - PARTS + 1)
                C.copy(hid_hi[:, w % PARTS, :], silu[:, q % 2, :]).then_inc(hid_hi_s, 1)

            def copy_out(b):
                act.wait_ge(parts_used, wide_chunk(b, CS - 1) + 1)
                if b > WIDE[0]:
                    act.wait_ge(job_done, block_job(b - 1) + 1)
                C.copy(turned_out[:, :], down_b[block_job(b) % 2][:, :]).then_inc(out_copied, 1)

            def round_weights(e, w):
                if w == 0:
                    act.wait_ge(ew_loaded[e % 2], 32 * (e // 2 + 1))
                    if e >= 2:
                        act.wait_ge(chunk_done, expert_chunk(e - 1))
                C.copy(ew_hi[:, e % 2, w, :], ew_raw[:, e % 2, w, :]).then_inc(ew_hi_s, 1)

            def slots_hi(e):
                act.wait_ge(xg_turned, e + 1)
                if e >= 2:
                    act.wait_ge(chunk_done, expert_chunk(e - 1))
                C.copy(xgT_hi[:, e % 2, :], turn_b[e % 2][:, 0:CAP]).then_inc(xg_hi_s, 1)

            def expert_out(e):
                act.wait_ge(job_done, expert_job(e) + 1)
                if e >= 2:
                    act.wait_ge(eo_written[e % 2], 48 * (e // 2))
                for r in range(3):
                    n = P if r < 2 else TAIL
                    last = C.activation(eo[0:n, e % 2, r, :], down_b[expert_job(e) % 2][0:n, D * r:D * r + D],
                                        ACT.Copy, scale=xg[0:n, e % XB, r, 0:1])
                last.then_inc(eo_ready, 1)

            def round_shared(i):
                cols = slice(2 * P * i, 2 * P * (i + 1))
                act.wait_ge(sw_loaded[2 * i * P // (IS // 2)], 32)
                C.copy(sw_hi[:, :, cols], sw_raw[:, :, cols]).then_inc(sw_hi_s, 1)

            root_of(PASSES[0])
            round_shared(0)
            normalize(0)
            root_of(PASSES[1])
            turned_hi(0)
            normalize(1)
            act.wait_ge(rwT_turned, 1)
            act.wait_ge(rwT_zeroed, 1)
            C.copy(rwT[:, B - 1, 0:E], rw_ps).then_inc(rwT_hi_s, 1)
            round_shared(1)
            turned_hi(1)
            root_of(PASSES[2])
            silu_chunk(0, S)
            normalize(2)
            normalize(3)
            silu_chunk(1, S)
            act.wait_ge(U_loaded, 16)
            for j in range(3):
                last = C.copy(U_hi[:, j, :], U_raw[:, :])
            last.then_inc(U_hi_s, 1)
            turned_hi(2)
            turned_hi(3)
            silu_chunk(2, S)
            round_shared(2)
            silu_chunk(3, S)
            act.wait_ge(lgT_done, B)
            C.copy(lgT[:, :], bank[4][:, :]).then_inc(lgT_copied, 1)
            round_shared(3)
            y_hi(0)
            silu_chunk(4, S)
            y_hi(1)
            silu_chunk(5, S)
            n_hi(0)
            silu_chunk(6, S)
            n_left(0)
            silu_chunk(7, S)
            act.wait_ge(e2_asked, 1)
            C.activation(e2[:, :], m2[:, :], ACT.Exp).then_inc(e2_ready, 1)
            exps(0)
            n_hi(1)
            y_hi(2)
            n_left(1)
            n_hi(2)
            y_hi(3)
            exps(1)
            n_left(2)
            n_hi(3)
            n_left(3)
            exps(2)
            round_weights(0, 0)
            round_weights(0, 1)
            act.wait_ge(sd_loaded, 16)
            exps(3)
            C.copy(sd_hi, sd[:, :, :]).then_inc(sd_hi_s, 1)
            for b in WIDE:
                for c in range(CS):
                    w = wide_chunk(b, c)
                    if w >= 1:
                        split_hi(w - 1)
                    silu_chunk(block_chunk(b) + c, S)
                    if c == 1 and b > WIDE[0]:
                        copy_out(b - 1)
                    if b == EARLY - 1:
                        if 3 <= c < 5:
                            round_weights(1, c - 3)
                        elif 5 <= c < 7:
                            slots_hi(c - 5)
            split_hi(wide_chunk(EARLY - 1, CS - 1))
            for e in range(E):
                for c in range(CR):
                    silu_chunk(expert_chunk(e) + c, CAP)
                    if e == 0 and c == 1:
                        copy_out(EARLY - 1)
                    if c == 1 and 1 <= e < E - 1:
                        slots_hi(e + 1)
                        round_weights(e + 1, 0)
                        round_weights(e + 1, 1)
                    if c == 1 and e >= 1:
                        expert_out(e - 1)
            for c in range(CS):
                silu_chunk(block_chunk(B - 1) + c, S)
                if c == 1:
                    expert_out(E - 1)

        @block.vector
        def _(dve):
            steps = [0]
            V = nc.vector

            def mark(ins):
                steps[0] += 1
                ins.then_inc(dve_step, 1)

            def settle():
                dve.wait_ge(dve_step, steps[0])

            def then(ins):
                mark(ins)
                settle()

            V.memset(fill[:, 0:1], 0.0)
            V.memset(fill[:, 2:RW], 0.0).then_inc(fill_zeroed, 1)
            V.memset(half[:, :], -0.5)
            V.memset(rwT[:, :, :].bitcast(F32), 0.0).then_inc(rwT_zeroed, 1)
            V.memset(ones_bf[:, :], 1.0).then_inc(ones_set, 1)
            V.memset(row1[:, :, RW:RW + 1], 1.0)

            def stats_of(g):
                dve.wait_ge(x_in_s[g], 16)
                for t in range(TG * g, TG * g + TG):
                    last = V.bn_stats(stats[:, t, :], acc[:, t, :])
                mark(last)

            def variances_of(gs):
                settle()
                ts = slice(TG * gs[0], TG * (gs[-1] + 1))
                for t in range(ts.start, ts.stop):
                    last = V.bn_aggr(mv[:, t, :], stats[:, t, :])
                then(last)
                V.tensor_scalar(ve[:, 0, ts], mv[:, ts, 1], LN_EPS, None, ALU.add)
                V.tensor_scalar(ve[:, 1, ts], mv[:, ts, 1], 1.0 + RMS_EPS, LN_EPS * RMS_EPS, ALU.mult, ALU.add
                                ).then_inc(ve_ready, 1)

            def rstd_of(gs):
                ts = slice(TG * gs[0], TG * (gs[-1] + 1))
                n = pass_of[gs[0]] + 1
                dve.wait_ge(root_ready, n)
                then(V.reciprocal(nw_a[:, :, ts], root[:, :, ts]))
                then(V.tensor_tensor(nw_b[:, :, ts], nw_a[:, :, ts], ve[:, :, ts], ALU.mult))
                then(V.scalar_tensor_tensor(out=nw_c[:, :, ts], in0=nw_b[:, :, ts], scalar=0.25,
                                            in1=root[:, :, ts], op0=ALU.mult, op1=ALU.add))
                V.reciprocal(rstd[:, :, ts], nw_c[:, :, ts]).then_inc(rstd_ready, 1)
                dve.wait_ge(rstd_ready, n)
                V.scalar_tensor_tensor(out=nmr[:, ts], in0=mv[:, ts, 0], scalar=-1.0, in1=rstd[:, 0, ts],
                                       op0=ALU.mult, op1=ALU.mult).then_inc(nmr_ready, 1)

            def normalize(g):
                for t in range(TG * g, TG * g + TG // 2):
                    last = V.tensor_scalar(xn[:, t, :], acc[:, t, :], mv[:, t, 0:1], rstd[:, 0, t:t + 1],
                                           ALU.subtract, ALU.mult)
                last.then_inc(xn_ready, 1)

            def turned_lo(g):
                cols = slice(S * g, S * g + S)
                dve.wait_ge(xnT_hi_s, g + 1)
                V.tensor_tensor(xnT_lo[:, cols], turn_b[g % 2][:, :], xnT_hi[:, cols].bitcast(F32),
                                ALU.subtract).then_inc(xnT_ready, 1)

            def per_token(ap):
                return ap.rearrange("p (t o) -> p t o", o=1).to_broadcast([P, NT, E])

            ids = e_ids[:, :].rearrange("p (o e) -> p o e", o=1).to_broadcast([P, NT, E])

            def route_logits():
                dve.wait_ge(lg_done, 1)
                then(V.tensor_tensor(z[:, :, :].rearrange("p (g j) e -> p j g e", g=B),
                                     lg_ps.rearrange("p (j g e) -> p j g e", j=TG, g=B),
                                     rms[:, :].rearrange("p (g j o) -> p j g o", g=B, o=1
                                                         ).to_broadcast([P, TG, B, E]), ALU.mult))
                mark(V.tensor_reduce(m1[:, :], z[:, :, :], AX_X, ALU.max))

            def route_best():
                settle()
                then(V.tensor_tensor(z2[:, :, :], z[:, :, :], per_token(m1[:, :]), ALU.subtract))
                then(V.tensor_scalar(z[:, :, :], z2[:, :, :], -87.5, None, ALU.max))
                mark(V.tensor_scalar(z2[:, :, :], z[:, :, :], 0.0, float(E), ALU.is_lt, ALU.mult))

            def route_first():
                settle()
                then(V.tensor_tensor(key[:, :, :], z2[:, :, :], ids, ALU.add))
                then(V.tensor_reduce(i1[:, :], key[:, :, :], AX_X, ALU.min))
                mark(V.tensor_tensor(chosen[:, 0, :, :], ids, per_token(i1[:, :]), ALU.is_equal))

            def route_next():
                settle()
                then(V.scalar_tensor_tensor(out=z2[:, :, :], in0=chosen[:, 0, :, :], scalar=-1000.0, in1=z[:, :, :],
                                            op0=ALU.mult, op1=ALU.add))
                V.tensor_reduce(m2[:, :], z2[:, :, :], AX_X, ALU.max).then_inc(e2_asked, 1)
                dve.wait_ge(e2_asked, 1)
                mark(V.tensor_tensor(key[:, :, :], z2[:, :, :], per_token(m2[:, :]), ALU.is_lt))

            def route_second():
                settle()
                then(V.scalar_tensor_tensor(out=z2[:, :, :], in0=key[:, :, :], scalar=float(E), in1=ids,
                                            op0=ALU.mult, op1=ALU.add))
                mark(V.tensor_reduce(i2[:, :], z2[:, :, :], AX_X, ALU.min))

            def route_chosen():
                settle()
                then(V.tensor_tensor(chosen[:, 1, :, :], ids, per_token(i2[:, :]), ALU.is_equal))
                V.tensor_tensor(sel[:, :, :].rearrange("p e t -> p t e"), chosen[:, 0, :, :], chosen[:, 1, :, :], ALU.add
                                ).then_inc(sel_ready, 1)

            def route_slots():
                flat = lambda a: a.rearrange("p e t -> p (e t)")
                dve.wait_ge(rank_done, 1)
                then(V.tensor_tensor_scan(flat(incl[:, :, :]), seg[:, :], tot_ps, 0.0, ALU.mult, ALU.add))
                V.tensor_tensor(pos[:, :, :], incl[:, :, :], rank_ps, ALU.add).then_inc(pos_ready, 1)
                dve.wait_ge(pos_ready, 1)
                then(V.tensor_tensor(over[:, :, :], pos[:, :, :], slot_end[:, :, :], ALU.is_ge))
                then(V.scalar_tensor_tensor(out=flat(slot[:, :, :]), in0=flat(over[:, :, :]),
                                            scalar=float(2 * NO_SLOT), in1=flat(pos[:, :, :]),
                                            op0=ALU.mult, op1=ALU.add))
                for k in range(2):
                    last = V.tensor_tensor(pick[:, k, :, :], chosen[:, k, :, :],
                                           slot[:, :, :].rearrange("p e t -> p t e"), ALU.mult)
                then(last)
                then(V.tensor_reduce(slot_f[:, :, :], pick[:, :, :, :], AX_X, ALU.add))
                V.tensor_scalar(slot_i[:, :, :], slot_f[:, :, :], float(NO_SLOT), None, ALU.min
                                ).then_inc(slots_ready, 1)

            def route_weights():
                dve.wait_ge(e2_ready, 1)
                then(V.tensor_scalar(e2p[:, :], e2[:, :], 1.0, None, ALU.add))
                then(V.reciprocal(row1[:, :, 0], e2p[:, :]))
                V.tensor_tensor(row2[:, :, 0], row1[:, :, 0], e2[:, :], ALU.mult).then_inc(wgt_ready, 1)

            def y_lo(g):
                cols = slice(S * g, S * g + S)
                ps = turn_b[g % 2]
                dve.wait_ge(y_hi_s, g + 1)
                V.tensor_tensor(yR[R:2 * R, cols], ps[R:2 * R, :], yL[R:2 * R, cols].bitcast(F32),
                                ALU.subtract)
                V.tensor_tensor(yL[2 * R:3 * R, cols], ps[2 * R:3 * R, :],
                                yR[2 * R:3 * R, cols].bitcast(F32), ALU.subtract)

            def n_lo(g):
                dve.wait_ge(nhi_ready, g + 1)
                V.scalar_tensor_tensor(out=norm_parts[NR, :], in0=norm_parts[NR, :].bitcast(F32),
                                       scalar=minus_lo[NR, 0:1], in1=turn_b[g % 2][NR, :],
                                       op0=ALU.mult, op1=ALU.add).then_inc(norm_split, 1)
                dve.wait_ge(norm_split, g + 1)
                V.tensor_scalar(yR[NR, S * g:S * g + S], norm_parts[NR, :].bitcast(F32),
                                first_two[NR, 0:1], last_two[NR, 0:1], ALU.mult, ALU.add).then_inc(y_ready, 1)

            def add_attention(b, h):
                dve.wait_ge(att_done, 2 * b + h + 1)
                o = down_b[h][:, 0:2 * (D + 1)].rearrange("p (r c) -> p r c", r=2)
                t = TG * b + 2 * h
                then(V.reciprocal(rden[:, t:t + 2], o[:, :, D]))
                for r in range(2):
                    last = V.scalar_tensor_tensor(out=acc[:, t + r, :], in0=o[:, r, 0:D],
                                                  scalar=rden[:, t + r:t + r + 1], in1=acc[:, t + r, :],
                                                  op0=ALU.mult, op1=ALU.add)
                last.then_inc(att_added, 1)

            def mult_chunk(q, n, hid):
                dve.wait_ge(silu_ready, q + 1)
                V.tensor_tensor(hid, up_b[q % 2][:, 0:n], silu[:, q % 2, 0:n], ALU.mult).then_inc(hid_ready, 1)

            def split_lo(w):
                q = block_chunk(WIDE[0]) + w
                dve.wait_ge(hid_hi_s, w + 1)
                V.tensor_tensor(hid_lo[:, w % PARTS, :], silu[:, q % 2, :],
                                hid_hi[:, w % PARTS, :].bitcast(F32), ALU.subtract).then_inc(hid_split, 1)

            def slots_lo(e):
                dve.wait_ge(xg_hi_s, e + 1)
                V.tensor_tensor(xgT_lo[:, e % 2, :], turn_b[e % 2][:, 0:CAP],
                                xgT_hi[:, e % 2, :].bitcast(F32), ALU.subtract).then_inc(xg_ready, 1)

            def block_sum(b):
                dve.wait_ge(job_done, block_job(b) + 1)
                if b > 0:
                    dve.wait_ge(att_added, 2 * (b + 1))
                a = acc[:, TG * b:TG * b + TG, :].rearrange("p t d -> p (t d)")
                source = turn_b[1] if b in WIDE else down_b[block_job(b) % 2]
                V.tensor_tensor(a, source[:, :], a, ALU.add).then_inc(block_added, 1)

            def last_block_sum(h):
                job = block_job(B - 1)
                dve.wait_ge(job_done, job + 1 + h)
                t = TG * (B - 1) + 2 * h
                a = acc[:, t:t + 2, :].rearrange("p t d -> p (t d)")
                V.tensor_tensor(a, down_b[(job + h) % 2][:, 0:2 * D], a, ALU.add).then_inc(block_added, 1)

            def mult_of_block(b, c):
                if b == B - 1 and c == 0:
                    dve.wait_ge(att_added, 2 * B)
                mult_chunk(block_chunk(b) + c, S, hid_s[:, b % 2, c, :])

            def add_routed(g):
                if g < B - 1:
                    dve.wait_ge(block_added, g + 1)
                dve.wait_ge(routed_loaded[g], 32)
                ts = slice(TG * g, TG * g + TG)
                then(V.tensor_tensor(acc[:, ts, :], routed[0][:, ts, :], acc[:, ts, :], ALU.add))
                V.tensor_tensor(acc[:, ts, :], routed[1][:, ts, :], acc[:, ts, :], ALU.add
                                ).then_inc(summed, 1)

            stats_of(0)
            variances_of(PASSES[0])
            stats_of(1)
            rstd_of(PASSES[0])
            normalize(0)
            variances_of(PASSES[1])
            stats_of(2)
            rstd_of(PASSES[1])
            turned_lo(0)
            normalize(1)
            stats_of(3)
            dve.wait_ge(rwT_hi_s, 1)
            V.tensor_tensor(rwT[:, B - 1, E:2 * E], rw_ps, rwT[:, B - 1, 0:E].bitcast(F32), ALU.subtract
                            ).then_inc(rwT_ready, 1)
            variances_of(PASSES[2])
            dve.wait_ge(consts, 1)
            V.tensor_copy(e_ids[:, :], e_ids_i[:, :])
            then(V.tensor_copy(slot0[:, :, :], slot0_i[:, :, :]))
            V.tensor_scalar(slot_end[:, :, :], slot0[:, :, :], float(CAP), None, ALU.add)
            by_row = ident[:, :].rearrange("p (g i e) -> p g i e", g=B, e=E)
            V.tensor_tensor(fold[:, :, :], by_row[:, :, 0, :], by_row[:, :, 1, :], ALU.add
                            ).then_inc(dve_const, 1)
            turned_lo(1)
            rstd_of(PASSES[2])
            normalize(2)
            mult_of_block(0, 0)
            normalize(3)
            dve.wait_ge(rstd_ready, len(PASSES))
            mark(V.tensor_tensor(std[:, :], ve[:, 0, :], rstd[:, 0, :], ALU.mult))
            mult_of_block(0, 1)
            settle()
            mark(V.tensor_tensor(rms[:, :], std[:, :], rstd[:, 1, :], ALU.mult))
            turned_lo(2)
            turned_lo(3)
            mult_of_block(0, 2)
            mult_of_block(0, 3)
            y_lo(0)
            settle()
            route_logits()
            route_best()
            mult_of_block(0, 4)
            route_first()
            mult_of_block(0, 5)
            n_lo(0)
            mult_of_block(0, 6)
            mult_of_block(0, 7)
            route_next()
            route_second()
            route_chosen()
            y_lo(1)
            n_lo(1)
            route_slots()
            route_weights()
            block_sum(0)
            dve.wait_ge(block_added, 1)
            y_lo(2)
            n_lo(2)
            y_lo(3)
            add_attention(0, 0)
            n_lo(3)
            add_attention(0, 1)
            for b in range(1, B):
                add_attention(b, 0)
                add_attention(b, 1)
                if b == B - 2:
                    dve.wait_ge(sd_hi_s, 1)
                    V.tensor_tensor(sd_lo, sd[:, :, :], sd_hi.bitcast(F32), ALU.subtract).then_inc(sd_split, 1)
            for b in WIDE:
                for c in range(CS):
                    q = block_chunk(b) + c
                    w = wide_chunk(b, c)
                    if w >= 1:
                        split_lo(w - 1)
                    mult_chunk(q, S, silu[:, q % 2, :])
                    if c == 3 and b > WIDE[0]:
                        block_sum(b - 1)
                    if b == EARLY - 1 and 5 <= c < 7:
                        slots_lo(c - 5)
            split_lo(wide_chunk(EARLY - 1, CS - 1))
            for e in range(E):
                if e >= 2:
                    dve.wait_ge(job_done, expert_job(e - 2) + 1)
                for c in range(CR):
                    mult_chunk(expert_chunk(e) + c, CAP, hid_e[:, e % 2, c, :])
                    if e == 1 and c == 0:
                        block_sum(EARLY - 1)
                    if c == 1 and 1 <= e < E - 1:
                        slots_lo(e + 1)
            for c in range(CS):
                mult_of_block(B - 1, c)
            for g in range(B):
                add_routed(g)
            dve.wait_ge(summed, B)
            last_block_sum(0)
            last_block_sum(1)

        @block.tensor
        def _(pe):
            M = nc.tensor.matmul

            def parts(o, w_hi, w_lo, m_hi, m_lo):
                M(o, w_hi, m_hi, start=True, stop=False)
                M(o, w_hi, m_lo, start=False, stop=False)
                return M(o, w_lo, m_hi, start=False, stop=True)

            def warm(n):
                with pe.Fori(0, n, 5):
                    for _ in range(5):
                        M(turn_b[1][:, 0:P], ones_bf[:, :], ones_bf[:, :], start=True, stop=True)

            def turn(g):
                pe.wait_ge(xn_ready, g + 1)
                pe.wait_ge(xn_ready_act, g + 1)
                if g >= 2:
                    pe.wait_ge(xnT_ready, g - 1)
                for j in range(TG):
                    last = nc.tensor.transpose(turn_b[g % 2][:, P * j:P * j + P], xn[:, TG * g + j, :],
                                               ident[:, :])
                last.then_inc(xnT_turned, 1)

            def logits(g):
                pe.wait_ge(xnT_ready, g + 1)
                cols = slice(S * g, S * g + S)
                w = rwT[:, B - 1 - g:2 * B - 1 - g, :].rearrange("p b c -> p (b c)")
                M(bank[4][:, :], w, xnT_hi[:, cols], start=(g == 0), stop=False)
                M(bank[4][:, :], w, xnT_lo[:, cols], start=False, stop=(g == B - 1)).then_inc(lgT_done, 1)

            def fold_logits():
                pe.wait_ge(lgT_copied, 1)
                for j in range(TG):
                    last = M(lg_ps[:, B * E * j:B * E * (j + 1)], lgT[:, P * j:P * j + P],
                             fold[:, :, :].rearrange("p g e -> p (g e)"), start=True, stop=True)
                last.then_inc(lg_done, 1)

            def project(g):
                cols = slice(S * g, S * g + S)
                if g < 2:
                    pe.wait_ge(xnT_ready, B + g - 1)
                else:
                    pe.wait_ge(y_ready, g - 1)
                parts(turn_b[g % 2][0:3 * R, :], U_hi[:, :, :].rearrange("p j r -> p (j r)"),
                      U_lo[:, :, :].rearrange("p j r -> p (j r)"), xnT_hi[:, cols], xnT_lo[:, cols]
                      ).then_inc(y_done, 1)

            def norms(g):
                pe.wait_ge(ysq_ready, g + 1)
                M(turn_b[g % 2][NR, :], half[:, :], ysq[:, S * g:S * g + S], start=True, stop=True
                  ).then_inc(n_done, 1)

            def scores(b):
                pe.wait_ge(y_ready, b + 1)
                pe.wait_ge(yL_ready, b + 1)
                for j in range(TG):
                    if b == 0:
                        pe.wait_ge(hid_ready, CS - 1 + j // 2)
                    else:
                        pe.wait_ge(prob_ready, TG * (b - 1) + j + 1)
                    M(bank[j][:, :], yL[0:3 * R + 4, S * b + P * j:S * b + P * j + P],
                      yR[0:3 * R + 4, S * b:S * b + S], start=True, stop=True).then_inc(score_done, 1)

            def attend(b, h):
                pe.wait_ge(prob_ready, TG * (b + 1))
                if b >= 1:
                    pe.wait_ge(att_added, 2 * (b - 1) + h + 1)
                elif h == 0:
                    pe.wait_ge(block_added, 1)
                else:
                    pe.wait_ge(pos_ready, 1)
                for i in range(2 * h, 2 * h + 2):
                    for j in range(TG):
                        last = M(down_b[h][:, (D + 1) * (i % 2):(D + 1) * (i % 2 + 1)],
                                 probs[:, b % 2, j, P * i:P * i + P], xn_ones[:, TG * b + j, :],
                                 start=(j == 0), stop=(j == TG - 1))
                last.then_inc(att_done, 1)

            def ranks():
                pe.wait_ge(sel_ready, 1)
                s = sel[:, :, :].rearrange("p e t -> p (e t)")
                M(bank[5][:, rank_cols], tri[:, :], s, start=True, stop=False)
                M(bank[5][:, rank_cols], ones_f[0:1, :], slot0[0:1, :, :].rearrange("p e t -> p (e t)"),
                  start=False, stop=True)
                M(tot_ps, ones_bf[:, :], s, start=True, stop=True).then_inc(rank_done, 1)

            def up_chunk(q, n, w_hi, w_lo, m_hi, m_lo):
                if q >= 2:
                    pe.wait_ge(silu_ready, q - 1)
                parts(gate_b[q % 2][:, 0:n], w_hi(0), w_lo(0), m_hi, m_lo)
                if q >= 2:
                    pe.wait_ge(hid_ready, q - 1)
                parts(up_b[q % 2][:, 0:n], w_hi(1), w_lo(1), m_hi, m_lo).then_inc(chunk_done, 1)

            def up_block(b, cs=range(CS)):
                pe.wait_ge(xnT_ready, b + 1)
                for c in cs:
                    if b == 0:
                        pe.wait_ge(sw_ready, c // 2 + 1)
                    up_chunk(block_chunk(b) + c, S, lambda w: sw_hi[:, w, P * c:P * c + P],
                             lambda w: sw_lo[:, w, P * c:P * c + P],
                             xnT_hi[:, S * b:S * b + S], xnT_lo[:, S * b:S * b + S])

            def bank_free(job):
                if job == 0:
                    pe.wait_ge(lgT_copied, 1)
                elif job <= 2:
                    pe.wait_ge(att_added, 2 * B)
                elif job - 2 < EARLY:
                    pe.wait_ge(block_added, job - 1)
                else:
                    pe.wait_ge(eo_ready, job - 1 - EARLY)

            def down_tile(o, b, i, cs=range(CS)):
                for c in cs:
                    last = M(o, hid_s[:, b % 2, c, P * i:P * i + P], sd[:, c, :],
                             start=(c == 0), stop=(c == CS - 1))
                return last

            def down_block(b, tiles=range(TG)):
                job = block_job(b)
                if 0 in tiles:
                    bank_free(job)
                    if b == 0:
                        pe.wait_ge(sd_loaded, 16)
                    pe.wait_ge(hid_ready, block_chunk(b) + CS)
                for i in tiles:
                    last = down_tile(down_b[job % 2][:, D * i:D * i + D], b, i)
                if TG - 1 in tiles:
                    last.then_inc(job_done, 1)

            def down_last_block():
                b = B - 1
                first, second = down_b[block_job(b) % 2], down_b[(block_job(b) + 1) % 2]
                bank_free(block_job(b))
                pe.wait_ge(hid_ready, block_chunk(b) + CS - 2)
                down_tile(first[:, 0:D], b, 0, range(CS - 2))
                pe.wait_ge(eo_ready, E)
                down_tile(second[:, 0:D], b, 2, range(CS - 2))
                pe.wait_ge(hid_ready, block_chunk(b) + CS)
                down_tile(first[:, 0:D], b, 0, range(CS - 2, CS))
                down_tile(first[:, D:2 * D], b, 1).then_inc(job_done, 1)
                down_tile(second[:, 0:D], b, 2, range(CS - 2, CS))
                down_tile(second[:, D:2 * D], b, 3).then_inc(job_done, 1)

            def down_wide(w):
                b, c = WIDE[0] + w // CS, w % CS
                o = down_b[block_job(b) % 2][:, :]
                if w == 0:
                    pe.wait_ge(sd_split, 1)
                if c == 0:
                    bank_free(block_job(b))
                pe.wait_ge(hid_split, w + 1)
                M(o, sd_hi[:, c, :], hid_hi[:, w % PARTS, :], start=(c == 0), stop=False)
                M(o, sd_hi[:, c, :], hid_lo[:, w % PARTS, :], start=False, stop=False)
                M(o, sd_lo[:, c, :], hid_hi[:, w % PARTS, :], start=False, stop=(c == CS - 1)
                  ).then_inc(parts_used, 1)

            def turn_out(b):
                pe.wait_ge(out_copied, b - WIDE[0] + 1)
                if b == WIDE[0]:
                    pe.wait_ge(y_ready, B)
                else:
                    pe.wait_ge(xg_ready, 2)
                for i in range(TG):
                    last = nc.tensor.transpose(turn_b[1][:, P * i:P * i + P],
                                               turned_out[:, P * i:P * i + P], ident[:, :])
                last.then_inc(job_done, 1)

            def turn_slots(e):
                s = e % 2
                pe.wait_ge(xg_loaded[s], 32 * (e // 2 + 1))
                if e == 1:
                    pe.wait_ge(block_added, EARLY - 1)
                elif e == 3:
                    pe.wait_ge(block_added, EARLY)
                elif e >= 2:
                    pe.wait_ge(xg_ready, e - 1)
                for r in range(3):
                    n = P if r < 2 else TAIL
                    last = nc.tensor.transpose(turn_b[s][:, P * r:P * r + n], xg[0:n, e % XB, r, 2:RW],
                                               ident[0:n, 0:n])
                last.then_inc(xg_turned, 1)

            def up_expert(e, cs=range(CR)):
                s = e % 2
                pe.wait_ge(ew_ready, e + 1)
                pe.wait_ge(xg_ready, e + 1)
                for c in cs:
                    up_chunk(expert_chunk(e) + c, CAP, lambda w: ew_hi[:, s, w, P * c:P * c + P],
                             lambda w: ew_lo[:, s, w, P * c:P * c + P], xgT_hi[:, s, :], xgT_lo[:, s, :])

            def down_expert(e):
                job = expert_job(e)
                bank_free(job)
                pe.wait_ge(rd_loaded[e % 3], 16 * (e // 3 + 1))
                pe.wait_ge(hid_ready, expert_chunk(e) + CR)
                for r in range(3):
                    n = P if r < 2 else TAIL
                    for c in range(CR):
                        last = M(down_b[job % 2][0:n, D * r:D * r + D], hid_e[:, e % 2, c, P * r:P * r + n],
                                 rd[:, e % 3, c, :], start=(c == 0), stop=(c == CR - 1))
                last.then_inc(job_done, 1)

            pe.wait_ge(ones_set, 1)
            warm(WARMING)
            pe.wait_ge(consts, 1)
            turn(0)
            pe.wait_ge(rw_loaded, 16)
            nc.tensor.transpose(rw_ps, rw_raw[:, :], ident[0:E, 0:E]).then_inc(rwT_turned, 1)
            warm(WARMING // 2)
            up_block(0, range(0, 1))
            turn(1)
            up_block(0, range(1, 2))
            pe.wait_ge(rwT_ready, 1)
            logits(0)
            logits(1)
            up_block(0, range(2, 3))
            turn(2)
            turn(3)
            up_block(0, range(3, 4))
            logits(2)
            logits(3)
            pe.wait_ge(U_ready, 1)
            project(0)
            pe.wait_ge(dve_const, 1)
            fold_logits()
            project(1)
            up_block(0, range(4, 5))
            norms(0)
            up_block(0, range(5, CS))
            norms(1)
            project(2)
            scores(0)
            down_block(0, range(0, 2))
            ranks()
            down_block(0, range(2, TG))
            norms(2)
            project(3)
            for b in range(B):
                if b + 1 < B:
                    scores(b + 1)
                attend(b, 0)
                if b == 0:
                    norms(3)
                attend(b, 1)
            for b in WIDE:
                for c in range(CS):
                    up_block(b, range(c, c + 1))
                    w = wide_chunk(b, c)
                    if w >= 2:
                        down_wide(w - 2)
                    if c == 2 and b > WIDE[0]:
                        turn_out(b - 1)
                    if b == EARLY - 1 and 4 <= c < 6:
                        turn_slots(c - 4)
            for c in range(2):
                up_expert(0, range(c, c + 1))
                down_wide(CS * len(WIDE) - 2 + c)
            up_expert(0, range(2, CR))
            turn_out(EARLY - 1)
            for e in range(1, E):
                if e < E - 1:
                    turn_slots(e + 1)
                up_expert(e, range(0, 2))
                down_expert(e - 1)
                up_expert(e, range(2, CR))
            up_block(B - 1, range(0, 2))
            down_expert(E - 1)
            up_block(B - 1, range(2, CS))
            down_last_block()


_INS = ['L0_attn_x', 'L0_attn_U', 'L0_ffn_router_w', 'L0_ffn_rg', 'L0_ffn_ru', 'L0_ffn_rd',
        'L0_ffn_sg', 'L0_ffn_su', 'L0_ffn_sd']
_OUTS = [((4, 512, 128), 'float32')]


def kernel(**inputs):
    import numpy as _np
    import concourse.bacc as _bacc
    from concourse import mybir as _mybir
    from concourse.bass_utils import run_bass_kernel_spmd as _run

    nc = _bacc.Bacc("TRN2", target_bir_lowering=False, num_devices=1)
    arrays, args = {}, []
    for name in _INS:
        a = _np.ascontiguousarray(inputs[name])
        arrays[f"in_{name}_dram"] = a
        args.append(nc.dram_tensor(f"in_{name}_dram", a.shape, _mybir.dt.from_np(a.dtype), kind="ExternalInput").ap())
    for i, (shape, dtype) in enumerate(_OUTS):
        dt = _mybir.dt.from_np(_np.dtype(dtype))
        args.append(nc.dram_tensor(f"out_{i}_dram", shape, dt, kind="ExternalOutput").ap())
    moe_attention_kernel(nc, *args)
    r = _run(nc, [arrays], core_ids=[0])
    got = tuple(r.results[0][f"out_{i}_dram"] for i in range(len(_OUTS)))
    return got[0]
```
